# Optimizing a Trainium2 kernel written in Bass

```python
import numpy as np
import jax
import jax.numpy as jnp

def _softmax(x, axis=-1):
    return jax.nn.softmax(x, axis=axis)

def _gelu(x):
    return jax.nn.gelu(x, approximate=True)

def _silu(x):
    return jax.nn.silu(x)

def _sigmoid(x):
    return jax.nn.sigmoid(x)

def _layernorm(x, axis=-1, eps=1e-05):
    m = jnp.mean(x, axis=axis, keepdims=True)
    v = jnp.var(x, axis=axis, keepdims=True)
    return (x - m) / jnp.sqrt(v + eps)

def _scatter_add(tgt, idx, src, axis=0):
    return tgt.at[idx].add(src)

def _segment_sum(src, seg, n):
    return jax.ops.segment_sum(src, seg, n)
kernel_name = 'mk_xattn_ffn_d1_seqx_r4_2ba1f2'

def setup_inputs(seed: int=0):
    np.random.seed(seed)
    _w = jnp.asarray

    def _rec_inputs():
        import jax
        import jax.numpy as jnp
        _rk = jax.random.key(seed)
        x = 6.313e-05 + 0.9998 * jax.random.normal(jax.random.fold_in(_rk, 1), (8, 512, 256), jnp.float32)
        _lenS = 512 - jax.random.randint(jax.random.fold_in(_rk, 7), (8,), 0, max(1, 512 // 4) + 1, jnp.int32)
        _lenS2 = 64 - jax.random.randint(jax.random.fold_in(_rk, 8), (8,), 0, max(1, 64 // 4) + 1, jnp.int32)
        _ctx_1024P = jax.random.normal(jax.random.fold_in(_rk, 11), (8, 16, 256), jnp.float32)
        _ctx_1024c = jax.random.dirichlet(jax.random.fold_in(_rk, 511), 0.3 * jnp.ones((16,), jnp.float32), (8, 64))
        _ctx_1024t = jnp.einsum('bsk,bkd->bsd', _ctx_1024c, _ctx_1024P)
        _ctx_1024t = _ctx_1024t * jax.lax.rsqrt(jnp.mean(jnp.square(_ctx_1024t)) + 1e-12) * 0.953939
        ctx_1024 = -0.000214406 + 1.00034 * (_ctx_1024t + 0.3 * jax.random.normal(jax.random.fold_in(_rk, 611), (8, 64, 256), jnp.float32))
        return (x, ctx_1024)
    x, ctx_1024 = _rec_inputs()

    def _L0_xattn_setup():
        import jax, jax.numpy as jnp
        import numpy as np
        from jax import lax
        BIG = jnp.float32(1e+30)

        def _pairwise_euclidean(a, b):
            aa = jnp.sum(a * a, axis=-1)[:, None]
            bb = jnp.sum(b * b, axis=-1)[None, :]
            ab = a @ b.T
            return jnp.sqrt(jnp.maximum(aa + bb - 2.0 * ab, 0.0))

        def _dtw_cost(D):
            row0 = jnp.cumsum(D[0])

            def row_step(prev_row, d_row):
                first = d_row[0] + prev_row[0]

                def col_step(left, inp):
                    d_ij, up, diag = inp
                    r = d_ij + jnp.minimum(jnp.minimum(up, left), diag)
                    return (r, r)
                _, rest = lax.scan(col_step, first, (d_row[1:], prev_row[1:], prev_row[:-1]))
                row = jnp.concatenate([first[None], rest])
                return (row, row)
            _, rows = lax.scan(row_step, row0, D[1:])
            return jnp.concatenate([row0[None], rows], axis=0)

        def _backtrack(R, T1, T2):
            L = T1 + T2 - 1

            def step(carry, _):
                i, j, done = carry
                valid = jnp.logical_not(done)
                cd = jnp.where((i > 0) & (j > 0), R[jnp.maximum(i - 1, 0), jnp.maximum(j - 1, 0)], BIG)
                cu = jnp.where(i > 0, R[jnp.maximum(i - 1, 0), j], BIG)
                cl = jnp.where(j > 0, R[i, jnp.maximum(j - 1, 0)], BIG)
                choice = jnp.argmin(jnp.stack([cd, cu, cl]))
                ni = jnp.where(choice <= 1, i - 1, i)
                nj = jnp.where((choice == 0) | (choice == 2), j - 1, j)
                at_origin = (i == 0) & (j == 0)
                ni = jnp.where(at_origin, 0, ni)
                nj = jnp.where(at_origin, 0, nj)
                return ((ni, nj, done | at_origin), (i, j, valid))
            init = (jnp.int32(T1 - 1), jnp.int32(T2 - 1), jnp.bool_(False))
            _, (i_idx, j_idx, valid) = lax.scan(step, init, None, length=L)
            return (i_idx, j_idx, valid)

        def _align_one(small, large):
            T_small, d = small.shape
            T_large = large.shape[0]
            D = _pairwise_euclidean(small, large)
            R = _dtw_cost(D)
            i_idx, j_idx, valid = _backtrack(R, T_small, T_large)
            contrib = small[i_idx] * valid[:, None].astype(small.dtype)
            expanded = jnp.zeros((T_large, d), dtype=small.dtype).at[j_idx].add(contrib)
            return expanded
        key = jax.random.key(seed)
        k1, k2 = jax.random.split(key)
        teacher = jax.random.normal(k1, (16, 100, 256), dtype=jnp.float32)
        student = jax.random.normal(k2, (16, 150, 256), dtype=jnp.float32)
        return {'teacher_features': teacher, 'student_features': student}
    _L0_xattn_all = _L0_xattn_setup()
    _L0_xattn_in = {k: v for k, v in _L0_xattn_all.items() if k in ()}
    del _L0_xattn_all

    def _L0_ffn_setup():
        import jax, jax.numpy as jnp
        import numpy as np

        def fixed_quant(x, width, frac_width):
            scale = jnp.float32(2.0 ** frac_width)
            imax = jnp.float32(2 ** (width - 1) - 1)
            imin = jnp.float32(-2 ** (width - 1))
            return jnp.clip(jnp.round(x * scale), imin, imax) / scale
        IN_F, HID_F, OUT_F = (256, 1024, 256)
        B, S = (4, 512)
        ACT_Q = (8, 4)
        W_Q = (8, 6)
        BIAS_Q = (8, 6)

        def quantized_linear(x, w, b):
            xq = fixed_quant(x, *ACT_Q)
            wq = fixed_quant(w, *W_Q)
            bq = fixed_quant(b, *BIAS_Q)
            return jnp.einsum('bsi,oi->bso', xq, wq) + bq

        def quantized_relu(x):
            return jax.nn.relu(fixed_quant(x, *ACT_Q))
        key = jax.random.key(seed)
        k_x, k_w1, k_b1, k_w2, k_b2 = jax.random.split(key, 5)
        x = jax.random.normal(k_x, (B, S, IN_F), dtype=jnp.float32)
        w1 = jax.random.normal(k_w1, (HID_F, IN_F), dtype=jnp.float32) / np.sqrt(IN_F)
        b1 = jax.random.normal(k_b1, (HID_F,), dtype=jnp.float32) / np.sqrt(IN_F)
        w2 = jax.random.normal(k_w2, (OUT_F, HID_F), dtype=jnp.float32) / np.sqrt(HID_F)
        b2 = jax.random.normal(k_b2, (OUT_F,), dtype=jnp.float32) / np.sqrt(HID_F)
        return {'x': x, 'w1': w1, 'b1': b1, 'w2': w2, 'b2': b2}
    _L0_ffn_all = _L0_ffn_setup()
    _L0_ffn_in = {k: v for k, v in _L0_ffn_all.items() if k in ('w1', 'b1', 'w2', 'b2')}
    del _L0_ffn_all
    return {'x': x, 'ctx_1024': ctx_1024, 'L0_ffn_w1': _L0_ffn_in['w1'], 'L0_ffn_b1': _L0_ffn_in['b1'], 'L0_ffn_w2': _L0_ffn_in['w2'], 'L0_ffn_b2': _L0_ffn_in['b2']}

def reference(x, ctx_1024, L0_ffn_w1, L0_ffn_b1, L0_ffn_w2, L0_ffn_b2):
    import jax
    import jax.numpy as jnp

    def _L0_xattn_ref(teacher_features, student_features):
        import jax, jax.numpy as jnp
        import numpy as np
        from jax import lax
        BIG = jnp.float32(1e+30)

        def _pairwise_euclidean(a, b):
            aa = jnp.sum(a * a, axis=-1)[:, None]
            bb = jnp.sum(b * b, axis=-1)[None, :]
            ab = a @ b.T
            return jnp.sqrt(jnp.maximum(aa + bb - 2.0 * ab, 0.0))

        def _dtw_cost(D):
            row0 = jnp.cumsum(D[0])

            def row_step(prev_row, d_row):
                first = d_row[0] + prev_row[0]

                def col_step(left, inp):
                    d_ij, up, diag = inp
                    r = d_ij + jnp.minimum(jnp.minimum(up, left), diag)
                    return (r, r)
                _, rest = lax.scan(col_step, first, (d_row[1:], prev_row[1:], prev_row[:-1]))
                row = jnp.concatenate([first[None], rest])
                return (row, row)
            _, rows = lax.scan(row_step, row0, D[1:])
            return jnp.concatenate([row0[None], rows], axis=0)

        def _backtrack(R, T1, T2):
            L = T1 + T2 - 1

            def step(carry, _):
                i, j, done = carry
                valid = jnp.logical_not(done)
                cd = jnp.where((i > 0) & (j > 0), R[jnp.maximum(i - 1, 0), jnp.maximum(j - 1, 0)], BIG)
                cu = jnp.where(i > 0, R[jnp.maximum(i - 1, 0), j], BIG)
                cl = jnp.where(j > 0, R[i, jnp.maximum(j - 1, 0)], BIG)
                choice = jnp.argmin(jnp.stack([cd, cu, cl]))
                ni = jnp.where(choice <= 1, i - 1, i)
                nj = jnp.where((choice == 0) | (choice == 2), j - 1, j)
                at_origin = (i == 0) & (j == 0)
                ni = jnp.where(at_origin, 0, ni)
                nj = jnp.where(at_origin, 0, nj)
                return ((ni, nj, done | at_origin), (i, j, valid))
            init = (jnp.int32(T1 - 1), jnp.int32(T2 - 1), jnp.bool_(False))
            _, (i_idx, j_idx, valid) = lax.scan(step, init, None, length=L)
            return (i_idx, j_idx, valid)

        def _align_one(small, large):
            T_small, d = small.shape
            T_large = large.shape[0]
            D = _pairwise_euclidean(small, large)
            R = _dtw_cost(D)
            i_idx, j_idx, valid = _backtrack(R, T_small, T_large)
            contrib = small[i_idx] * valid[:, None].astype(small.dtype)
            expanded = jnp.zeros((T_large, d), dtype=small.dtype).at[j_idx].add(contrib)
            return expanded
        return jax.vmap(_align_one)(teacher_features, student_features)

    def _L0_ffn_ref(x, w1, b1, w2, b2):
        import jax, jax.numpy as jnp
        import numpy as np

        def fixed_quant(x, width, frac_width):
            scale = jnp.float32(2.0 ** frac_width)
            imax = jnp.float32(2 ** (width - 1) - 1)
            imin = jnp.float32(-2 ** (width - 1))
            return jnp.clip(jnp.round(x * scale), imin, imax) / scale
        IN_F, HID_F, OUT_F = (256, 1024, 256)
        B, S = (4, 512)
        ACT_Q = (8, 4)
        W_Q = (8, 6)
        BIAS_Q = (8, 6)

        def quantized_linear(x, w, b):
            xq = fixed_quant(x, *ACT_Q)
            wq = fixed_quant(w, *W_Q)
            bq = fixed_quant(b, *BIAS_Q)
            return jnp.einsum('bsi,oi->bso', xq, wq) + bq

        def quantized_relu(x):
            return jax.nn.relu(fixed_quant(x, *ACT_Q))
        h = quantized_linear(x, w1, b1)
        h = quantized_relu(h)
        out = quantized_linear(h, w2, b2)
        return out
    x = x + _L0_xattn_ref(ctx_1024, _layernorm(x, axis=-1))
    x = x + _L0_ffn_ref(_layernorm(x, axis=-1), L0_ffn_w1, L0_ffn_b1, L0_ffn_w2, L0_ffn_b2)
    return x

_drawn_inputs = setup_inputs


def setup_inputs(seed=0):
    import zlib

    import numpy as np

    out = dict(_drawn_inputs(seed))
    spreads = {}
    factors = {'L0_ffn_b2': 2.699}
    for name, (base, spread) in spreads.items():
        noise = np.random.default_rng([zlib.crc32(name.encode()), seed]).standard_normal(out[name].shape)
        drawn = base * np.exp(spread * noise) if base else spread * noise
        out[name] = jnp.asarray(drawn.astype(out[name].dtype))
    for name, factor in factors.items():
        out[name] = (out[name] * factor).astype(out[name].dtype)
    return out
```

```python
import concourse.bass as bass
from concourse import mybir
from contextlib import ExitStack

BIG = 1e30
B, T, D = 8, 512, 256
I = 64
HID = 1024
P = 128
W = 32
CH = T // W
NQ = P // W
NU = 2 * CH
SLOTS = I + CH - 1
KH = D // P
EPS = 1e-5
LOADS = 4
UL = NU // LOADS
NG = NU // 4
NH = HID // P
OT = D // P
ACT_ONE, W_ONE = 16.0, 64.0
QMAX, QMIN = 127.0, -128.0


def align_ffn_kernel(nc: bass.Bass, x, ctx_in, w1, b1, w2, b2, out):
    f32, bf16, i16 = mybir.dt.float32, mybir.dt.bfloat16, mybir.dt.int16
    ALU, ACT = mybir.AluOpType, mybir.ActivationFunctionType

    x_v = x.rearrange("(q h) (c w) d -> q h w c d", h=2, w=W)
    out_v = out.rearrange("(q h) (c w) d -> q h w c d", h=2, w=W)
    ctx_v = ctx_in.rearrange("(q h) i d -> (h i) q d", h=2)

    with ExitStack() as ctx:
        def sb(name, shape, dt=f32):
            return ctx.enter_context(nc.sbuf_tensor(name, shape, dt))

        def bank(name, shape, dt=f32):
            return ctx.enter_context(nc.psum_tensor(name, shape, dt))

        def sem(name):
            return ctx.enter_context(nc.semaphore(name))

        X = sb("X", [P, NU, D])
        Xn = sb("Xn", [P, 2, UL, D])
        XnT = sb("XnT", [P, 2, UL, KH, P])
        stats = sb("stats", [P, NU, 6])
        mv = sb("mv", [P, NU, 2])
        std = sb("std", [P, NU])
        rstd = sb("rstd", [P, NU])
        vr = sb("vr", [P, NU])
        bb = sb("bb", [P, NU])
        S = sb("S", [P, NQ, D])
        S_hi = sb("S_hi", [P, NQ, D], bf16)
        S_mid = sb("S_mid", [P, NQ, D], bf16)
        S_lo = sb("S_lo", [P, NQ, D], bf16)
        ST = sb("ST", [P, NQ, KH, P])
        ST2 = sb("ST2", [P, NQ, KH, P])
        S_r1 = ST2[:, :, :, :].rearrange("p q k n -> p q (k n)")
        aa = sb("aa", [P, 2, I])
        norms = sb("norms", [P, LOADS, UL, I])
        E = sb("E", [P, SLOTS, NU])
        Dm = sb("Dm", [P, SLOTS, W + 1])
        M = sb("M", [P, SLOTS, W + 1])
        R = sb("R", [P, SLOTS + 1, W + 1])
        carry = sb("carry", [P, SLOTS + 1])
        init0 = sb("init0", [P, 1])
        LC = sb("LC", [P, SLOTS, W, 2], bf16)
        A = sb("A", [P, SLOTS, W], bf16)
        UD = sb("UD", [P, SLOTS, W, 2], bf16)
        enter = sb("enter", [P, 2, W, 2], bf16)
        BK = sb("BK", [P, SLOTS, W, 2], bf16)
        bcarry = sb("bcarry", [P, SLOTS + 1], bf16)
        PT = A
        chunk0 = sb("chunk0", [P, B])
        chunk15 = sb("chunk15", [P, B])
        first = sb("first", [P, 1])
        last = sb("last", [P, 1])
        ident = sb("ident", [P, P])
        ident_bf = sb("ident_bf", [P, P], bf16)
        flip = sb("flip", [P, P], bf16)
        ones = sb("ones", [P, W])
        w1_raw = sb("w1_raw", [P, NH, D])
        w2_raw = sb("w2_raw", [P, OT, HID])
        w_int = sb("w_int", [P, 2, NH * D], i16)
        w1_q = w1_raw[:, :, :].rearrange("p n d -> p (n d)").bitcast(bf16)[:, 0:NH * D].rearrange(
            "p (n d) -> p n d", d=D)
        w2_q = w2_raw[:, :, :].rearrange("p n d -> p (n d)").bitcast(bf16)[:, 0:OT * HID].rearrange(
            "p (n d) -> p n d", d=HID)
        w1T = sb("w1T", [P, KH, HID], bf16)
        w2T = sb("w2T", [P, NH, D], bf16)
        b1_raw = sb("b1_raw", [P, NH])
        b1_int = sb("b1_int", [P, NH], i16)
        b1_q = sb("b1_q", [P, NH])
        b1_s = sb("b1_s", [P, NH])
        b2_raw = sb("b2_raw", [P, D])
        b2_int = sb("b2_int", [P, D], i16)
        b2_q = sb("b2_q", [P, D])
        b2_s = sb("b2_s", [P, D])
        PB = sb("PB", [P, 2, 2, P], bf16)
        stats2 = sb("stats2", [P, NU, 6])
        mv2 = sb("mv2", [P, NU, 2])
        std2 = sb("std2", [P, NU])
        rstd2 = sb("rstd2", [P, NU])
        rs16 = sb("rs16", [P, NU])
        xq_both = Dm[:, :, :].rearrange("p s w -> p (s w)")[:, 0:4 * D * 2]
        xq_int = xq_both[:, 0:4 * D].bitcast(i16).rearrange("p (a t d) -> p a t d", a=2, t=4)
        xq = xq_both[:, 4 * D:8 * D].bitcast(bf16).rearrange("p (a t d) -> p a t d", a=2, t=4)
        xqT = M[:, :, :].rearrange("p s w -> p (s w)")[:, 0:KH * 4 * P].bitcast(bf16).rearrange(
            "p (a k n) -> p a k n", a=2, k=KH)
        h_int = Xn[:, :, :, :].rearrange("p a u d -> p (a u d)").bitcast(i16).rearrange(
            "p (a n t) -> p a n t", a=2, n=NH)
        hq = XnT[:, :, :, :, :].rearrange("p a u k d -> p (a u k d)").bitcast(bf16).rearrange(
            "p (a n t) -> p a n t", a=2, n=NH)
        res = E[:, :, :].rearrange("p s u -> p (s u)")[:, 0:8 * D].rearrange("p (a t d) -> p a t d", a=2, t=4)

        bank01 = [bank("h0", [P, 512]), bank("h1", [P, 512])]
        bank23 = [bank("e0", [P, 2, D]), bank("e1", [P, 2, D])]
        bank4 = bank("t4", [P, 2, 4 * P], bf16)
        bank5 = bank("t5", [P, 512])
        bank67 = [bank("y0", [P, 2, D]), bank("y1", [P, 2, D])]
        path_ps = bank5[:, :].bitcast(bf16)
        flat4 = bank4[:, :, :].rearrange("p a b -> p (a b)")

        x_in = [sem(f"x_in{k}") for k in range(LOADS)]
        ctx_loaded = sem("ctx_loaded")
        w_loaded = sem("w_loaded")
        out_stored = [[sem(f"out_stored{a}{h}") for h in range(2)] for a in range(2)]
        ident_made = sem("ident_made")
        pool_const = sem("pool_const")
        norms_made = sem("norms_made")
        clamped = sem("clamped")
        ctx_split = sem("ctx_split")
        w_clip = sem("w_clip")
        biased = sem("biased")
        dve = sem("dve")
        var_ready = sem("var_ready")
        bb_ready = sem("bb_ready")
        xn_ready = sem("xn_ready")
        dist2_ready = sem("dist2_ready")
        step_done = sem("step_done")
        back_done = sem("back_done")
        path_ready = sem("path_ready")
        x1_ready = sem("x1_ready")
        var2_ready = sem("var2_ready")
        quant_read = sem("quant_read")
        xq_ready = sem("xq_ready")
        hq_ready = sem("hq_ready")
        res_ready = sem("res_ready")
        std_ready = sem("std_ready")
        ctxT_copied = sem("ctxT_copied")
        ctx_sq = sem("ctx_sq")
        aa_copied = sem("aa_copied")
        xT_copied = sem("xT_copied")
        rooted = sem("rooted")
        w_rounded = sem("w_rounded")
        wT_copied = sem("wT_copied")
        path_copied = sem("path_copied")
        std2_ready = sem("std2_ready")
        xqT_copied = sem("xqT_copied")
        h_rounded = sem("h_rounded")
        ctxT_done = sem("ctxT_done")
        aa_done = sem("aa_done")
        xT_done = sem("xT_done")
        dot_done = sem("dot_done")
        wT_done = sem("wT_done")
        pathT_done = sem("pathT_done")
        aligned = sem("aligned")
        xqT_done = sem("xqT_done")
        h_done = sem("h_done")
        y_done = sem("y_done")

        def load_of(k):
            return k // 2, (k % 2) * UL, k * UL

        def chunk_of(g):
            return CH - 2 - 2 * g

        dist_banks = [bank23[0], bank23[1], bank67[0], bank67[1]]

        block = ctx.enter_context(nc.Block())

        @block.sync
        def _(sp):
            sp.dma_start(S[:, :, :], ctx_v).then_inc(ctx_loaded, 16)
            for k in range(LOADS):
                h, c0, u0 = load_of(k)
                for q in range(NQ):
                    sp.dma_start(X[W * q:W * q + W, u0:u0 + UL, :], x_v[q, h, :, c0:c0 + UL, :]).then_inc(x_in[k], 16)
            sp.dma_start(w1_raw[:, :, :], w1.rearrange("(p n) d -> p n d", n=NH)).then_inc(w_loaded, 16)
            sp.dma_start(w2_raw[:, :, :], w2.rearrange("(n p) d -> p n d", p=P)).then_inc(w_loaded, 16)
            sp.dma_start(b2_raw[:, :], b2.partition_broadcast(P)).then_inc(w_loaded, 16)
            sp.dma_start(b1_raw[:, :], b1.rearrange("(p n) -> p n", n=NH)).then_inc(w_loaded, 16)
            for g in range(NG):
                c0 = chunk_of(g)
                for h in range(2):
                    sp.wait_ge(res_ready, 2 * g + h + 1)
                    for q in range(NQ):
                        sp.dma_start(out_v[q, h, :, c0:c0 + 2, :],
                                     res[W * q:W * q + W, g % 2, 2 * h:2 * h + 2, :]).then_inc(out_stored[g % 2][h], 16)
            for a in range(2):
                for h in range(2):
                    sp.wait_ge(out_stored[a][h], 16 * NQ * (NG // 2))

        @block.gpsimd
        def _(pool):
            nc.gpsimd.memset(ident[:, :], 0.0).then_inc(ident_made, 1)
            pool.wait_ge(ident_made, 1)
            nc.gpsimd.affine_select(out=ident[:, :], in_=ident[:, :], compare_op=ALU.not_equal, fill=1.0, base=0,
                                    pattern=[[-1, P]], channel_multiplier=1).then_inc(ident_made, 1)
            nc.gpsimd.memset(ones[:, :], 1.0).then_inc(pool_const, 1)
            nc.gpsimd.memset(ident_bf[:, :], 0.0).then_inc(pool_const, 1)
            nc.gpsimd.memset(flip[:, :], 0.0).then_inc(pool_const, 1)
            nc.gpsimd.memset(chunk0[:, :], 0.0).then_inc(pool_const, 1)
            nc.gpsimd.memset(chunk15[:, :], 0.0).then_inc(pool_const, 1)
            nc.gpsimd.memset(E[:, :, :], 0.0).then_inc(pool_const, 1)
            pool.wait_ge(pool_const, 6)
            nc.gpsimd.affine_select(out=ident_bf[:, :], in_=ident_bf[:, :], compare_op=ALU.not_equal, fill=1.0,
                                    base=0, pattern=[[-1, P]], channel_multiplier=1).then_inc(pool_const, 1)
            nc.gpsimd.affine_select(out=flip[:, :].rearrange("p (a b) -> p a b", b=W),
                                    in_=flip[:, :].rearrange("p (a b) -> p a b", b=W),
                                    compare_op=ALU.not_equal, fill=1.0, base=-(W - 1),
                                    pattern=[[-W, NQ], [1, W]], channel_multiplier=1).then_inc(pool_const, 1)
            for t, off in ((chunk0, 0), (chunk15, CH - 1)):
                nc.gpsimd.affine_select(out=t[:, :], in_=t[:, :], compare_op=ALU.not_equal, fill=1.0, base=-off,
                                        pattern=[[-CH, B]], channel_multiplier=1).then_inc(pool_const, 1)
            nc.gpsimd.memset(Dm[:, 0, 0:1], 0.0).then_inc(pool_const, 1)
            nc.gpsimd.memset(Dm[:, 1:SLOTS, 0:1], 0.0).then_inc(pool_const, 1)
            nc.gpsimd.memset(M[:, :, 0:1], BIG).then_inc(pool_const, 1)
            nc.gpsimd.memset(R[:, 0, :], BIG).then_inc(pool_const, 1)
            nc.gpsimd.memset(R[:, 1, 0:1], BIG).then_inc(pool_const, 1)
            nc.gpsimd.memset(LC[:, :, :, 0], 1.0).then_inc(pool_const, 1)
            nc.gpsimd.memset(enter[:, 0, :, :], 0.0).then_inc(pool_const, 1)

            for k in range(LOADS):
                h, c0, u0 = load_of(k)
                pool.wait_ge(aa_copied, 1)
                pool.wait_ge(bb_ready, k + 1)
                nc.gpsimd.tensor_tensor(norms[:, k, :, :], aa[:, h:h + 1, :].to_broadcast([P, UL, I]),
                                        bb[:, u0:u0 + UL].unsqueeze(2).to_broadcast([P, UL, I]),
                                        ALU.add).then_inc(norms_made, 1)
                pool.wait_ge(dist2_ready, k + 1)
                nc.gpsimd.tensor_scalar(norms[:, k, :, :], norms[:, k, :, :], 0.0, 1.0, ALU.max,
                                        ALU.mult).then_inc(clamped, 1)

            pool.wait_ge(ctx_loaded, 16)
            nc.gpsimd.tensor_copy(S_hi[:, :, :], S[:, :, :]).then_inc(ctx_split, 1)
            pool.wait_ge(ctx_split, 1)
            pool.wait_ge(aa_done, 1)
            nc.gpsimd.tensor_tensor(S_r1[:, :, :], S[:, :, :], S_hi[:, :, :], ALU.subtract).then_inc(ctx_split, 1)
            pool.wait_ge(ctx_split, 2)
            nc.gpsimd.tensor_copy(S_mid[:, :, :], S_r1[:, :, :]).then_inc(ctx_split, 1)
            pool.wait_ge(ctx_split, 3)
            nc.gpsimd.tensor_tensor(S_lo[:, :, :], S_r1[:, :, :], S_mid[:, :, :], ALU.subtract).then_inc(ctx_split, 1)

            pool.wait_ge(w_rounded, 4)
            nc.gpsimd.tensor_scalar(w1_q[:, :, :].rearrange("p n d -> p (n d)"), w_int[:, 0, :], QMAX, QMIN, ALU.min,
                                    ALU.max).then_inc(w_clip, 1)
            nc.gpsimd.tensor_scalar(w2_q[:, :, :].rearrange("p n d -> p (n d)"), w_int[:, 1, :], QMAX, QMIN, ALU.min,
                                    ALU.max).then_inc(w_clip, 1)
            nc.gpsimd.tensor_scalar(b1_q[:, :], b1_int[:, :], QMAX, QMIN, ALU.min, ALU.max).then_inc(w_clip, 1)
            nc.gpsimd.tensor_scalar(b2_q[:, :], b2_int[:, :], QMAX, QMIN, ALU.min, ALU.max).then_inc(w_clip, 1)
            pool.wait_ge(w_clip, 4)
            nc.gpsimd.tensor_scalar(b1_s[:, :], b1_q[:, :], ACT_ONE / W_ONE, 0.0, ALU.mult, ALU.add).then_inc(w_clip, 1)
            nc.gpsimd.tensor_scalar(b2_s[:, :], b2_q[:, :], 1.0 / W_ONE, 0.0, ALU.mult, ALU.add).then_inc(w_clip, 1)
            pool.wait_ge(w_clip, 6)

            for g in range(NG):
                c0 = chunk_of(g)
                pool.wait_ge(quant_read, g + 1)
                for h in range(2):
                    v = X[:, CH * h + c0:CH * h + c0 + 2, :]
                    nc.gpsimd.tensor_tensor(v, v, b2_s[:, :].unsqueeze(1).to_broadcast([P, 2, D]),
                                            ALU.add).then_inc(biased, 1)

        @block.scalar
        def _(act):
            for b in range(2):
                act.wait_ge(ctxT_done, b + 1)
                nc.scalar.activation(ST[:, 2 * b:2 * b + 2, :, :].rearrange("p q k n -> p (q k n)"), bank01[b][:, :],
                                     ACT.Copy).then_inc(ctxT_copied, 1)
                act.wait_ge(ctxT_copied, b + 1)
                nc.scalar.activation(ST2[:, 2 * b:2 * b + 2, :, :], ST[:, 2 * b:2 * b + 2, :, :],
                                     ACT.Square).then_inc(ctx_sq, 1)
            act.wait_ge(aa_done, 1)
            nc.scalar.activation(aa[:, :, :].rearrange("p h i -> p (h i)"), bank5[:, 0:P], ACT.Copy).then_inc(aa_copied, 1)

            def roots(k):
                h, c0, u0 = load_of(k)
                act.wait_ge(clamped, k + 1)
                act.wait_ge(pool_const, 6)
                dst = bass.AP(E, c0 * NU + u0, [[SLOTS * NU, P], [NU + 1, UL], [NU, I]])
                nc.scalar.activation(dst, norms[:, k, :, :], ACT.Sqrt).then_inc(rooted, 1)

            for k in range(LOADS):
                h, c0, u0 = load_of(k)
                act.wait_ge(var_ready, k + 1)
                nc.scalar.activation(std[:, u0:u0 + UL], vr[:, u0:u0 + UL], ACT.Sqrt).then_inc(std_ready, 1)
                for j in range(UL // 2):
                    n = k * (UL // 2) + j
                    act.wait_ge(xT_done, n + 1)
                    if k >= 2 and j == 0:
                        act.wait_ge(dot_done, k - 1)
                    nc.scalar.activation(XnT[:, k % 2, 2 * j:2 * j + 2, :, :].rearrange("p u k n -> p (u k n)"),
                                         bank01[n % 2][:, :], ACT.Copy).then_inc(xT_copied, 1)
                if k >= 1:
                    roots(k - 1)
            roots(LOADS - 1)

            act.wait_ge(w_loaded, 64)
            nc.scalar.activation(w_int[:, 0, :], w1_raw[:, :, :].rearrange("p n d -> p (n d)"), ACT.Copy,
                                 scale=W_ONE).then_inc(w_rounded, 1)
            nc.scalar.activation(w_int[:, 1, :], w2_raw[:, :, :].rearrange("p n d -> p (n d)"), ACT.Copy,
                                 scale=W_ONE).then_inc(w_rounded, 1)
            nc.scalar.activation(b1_int[:, :], b1_raw[:, :], ACT.Copy, scale=W_ONE).then_inc(w_rounded, 1)
            nc.scalar.activation(b2_int[:, :], b2_raw[:, :], ACT.Copy, scale=W_ONE).then_inc(w_rounded, 1)
            for n in range(NH):
                act.wait_ge(wT_done, n + 1)
                src = (flat4, path_ps)[n % 2][:, 0:512]
                if n < NH // 2:
                    dst = w1T[:, :, 2 * n * P:2 * n * P + 2 * P].rearrange("p k (m n) -> p m k n", m=2)
                    src = src.rearrange("p (m k n) -> p m k n", m=2, k=KH)
                else:
                    m = n - NH // 2
                    dst = w2T[:, 2 * m:2 * m + 2, :].rearrange("p m n -> p (m n)")
                nc.scalar.activation(dst, src, ACT.Copy).then_inc(wT_copied, 1)

            def copy_path(g):
                act.wait_ge(pathT_done, g + 1)
                if g >= 2:
                    act.wait_ge(aligned, 2 * (g - 1))
                nc.scalar.activation(PB[:, g % 2, :, :].rearrange("p j n -> p (j n)"), path_ps[:, 0:2 * P],
                                     ACT.Copy).then_inc(path_copied, 1)

            def deviation(g):
                act.wait_ge(var2_ready, g + 1)
                nc.scalar.activation(std2[:, 4 * g:4 * g + 4], rs16[:, 4 * g:4 * g + 4], ACT.Sqrt).then_inc(std2_ready, 1)

            def copy_xqT(g):
                act.wait_ge(xqT_done, g + 1)
                if g >= 2:
                    act.wait_ge(h_done, NH * (g - 1))
                nc.scalar.activation(xqT[:, g % 2, :, :], bank4[:, :, :], ACT.Copy).then_inc(xqT_copied, 1)

            def round_hidden(g, n):
                act.wait_ge(h_done, NH * g + n + 1)
                if g >= 2 and n == 0:
                    act.wait_ge(hq_ready, NH * (g - 1))
                nc.scalar.activation(h_int[:, g % 2, n, :], bank01[n % 2][:, :], ACT.Identity, bias=b1_s[:, n:n + 1],
                                     scale=1.0 / W_ONE).then_inc(h_rounded, 1)

            copy_path(0)
            deviation(0)
            copy_path(1)
            act.wait_ge(w_clip, 6)
            copy_xqT(0)
            for n in range(NH):
                if n == NH // 2:
                    deviation(1)
                round_hidden(0, n)
            for g in range(NG):
                if g + 2 < NG:
                    copy_path(g + 2)
                if g + 1 < NG:
                    copy_xqT(g + 1)
                    for n in range(NH):
                        if n == NH // 2 and g + 2 < NG:
                            deviation(g + 2)
                        round_hidden(g + 1, n)

        @block.vector
        def _(v):
            own = [0]

            def link(ins):
                own[0] += 1
                ins.then_inc(dve, 1)
                v.wait_ge(dve, own[0])

            v.wait_ge(pool_const, 17)
            nc.vector.reduce_max(first[:, :], chunk0[:, :], mybir.AxisListType.X).then_inc(dve, 1)
            nc.vector.reduce_max(last[:, :], chunk15[:, :], mybir.AxisListType.X).then_inc(dve, 1)
            own[0] += 2
            v.wait_ge(dve, own[0])
            nc.vector.tensor_scalar(init0[:, :], first[:, :], -BIG, BIG, ALU.mult, ALU.add).then_inc(dve, 1)
            nc.vector.tensor_scalar(Dm[:, 1:SLOTS, 0], Dm[:, 1:SLOTS, 0], 1.0, first[:, :], ALU.mult,
                                    ALU.add).then_inc(dve, 1)
            nc.vector.tensor_copy(bcarry[:, SLOTS:SLOTS + 1], last[:, :]).then_inc(dve, 1)
            own[0] += 3
            v.wait_ge(dve, own[0])
            link(nc.vector.tensor_scalar(Dm[:, 1:SLOTS, 0], Dm[:, 1:SLOTS, 0], BIG, None, ALU.mult))

            def distances(k):
                v.wait_ge(dot_done, k + 1)
                v.wait_ge(norms_made, k + 1)
                nc.vector.scalar_tensor_tensor(out=norms[:, k, :, :].rearrange("p u i -> p (u i)"),
                                               in0=dist_banks[k][:, :, :].rearrange("p a b -> p (a b)"), scalar=-2.0,
                                               in1=norms[:, k, :, :].rearrange("p u i -> p (u i)"),
                                               op0=ALU.mult, op1=ALU.add).then_inc(dist2_ready, 1)

            for k in range(LOADS):
                h, c0, u0 = load_of(k)
                us = slice(u0, u0 + UL)
                v.wait_ge(x_in[k], 16 * NQ)
                for u in range(u0, u0 + UL):
                    nc.vector.bn_stats(stats[:, u, :], X[:, u, :]).then_inc(dve, 1)
                own[0] += UL
                v.wait_ge(dve, own[0])
                for u in range(u0, u0 + UL):
                    nc.vector.bn_aggr(mv[:, u, :], stats[:, u, :]).then_inc(dve, 1)
                own[0] += UL
                v.wait_ge(dve, own[0])
                nc.vector.tensor_scalar(vr[:, us], mv[:, us, 1], EPS, None, ALU.add).then_inc(var_ready, 1)
                v.wait_ge(std_ready, k + 1)
                link(nc.vector.reciprocal(rstd[:, us], std[:, us]))
                link(nc.vector.tensor_tensor(bb[:, us], mv[:, us, 1], rstd[:, us], ALU.mult))
                if k >= 2:
                    v.wait_ge(xT_done, (UL // 2) * (k - 1))
                for j in range(UL):
                    nc.vector.tensor_scalar(Xn[:, k % 2, j, :], X[:, u0 + j, :], mv[:, u0 + j, 0:1],
                                            rstd[:, u0 + j:u0 + j + 1], ALU.subtract, ALU.mult).then_inc(xn_ready, 1)
                    if j == 0:
                        nc.vector.scalar_tensor_tensor(out=bb[:, us], in0=bb[:, us], scalar=float(D),
                                                       in1=rstd[:, us], op0=ALU.mult, op1=ALU.mult).then_inc(bb_ready, 1)
                if k >= 1:
                    distances(k - 1)
            distances(LOADS - 1)

            v.wait_ge(rooted, LOADS)
            link(nc.vector.transpose(Dm[:, :, 1:W + 1], E[:, :, :]))

            right = [W - 1] + list(range(W - 1))
            left = list(range(1, W)) + [0]
            n = 0

            def go_left(s):
                return nc.vector.tensor_tensor(LC[:, s, :, 1], M[:, s, W:0:-1], R[:, s + 1, W - 1::-1], ALU.is_gt)

            def diagonal(s):
                return nc.vector.tensor_tensor(A[:, s, :], R[:, s, W - 1::-1], M[:, s, W:0:-1], ALU.is_le)

            scan_at = []
            for s in range(SLOTS):
                if s:
                    v.wait_ge(step_done, scan_at[s - 1])
                nc.vector.tensor_tensor(M[:, s, 1:W + 1], R[:, s, 1:W + 1], R[:, s, 0:W], ALU.min).then_inc(step_done, 1)
                n += 1
                if s:
                    nc.vector.stream_shuffle(carry[:, s:s + 1], R[:, s, W:W + 1], right).then_inc(step_done, 1)
                    n += 1
                ready = n
                if s >= 2:
                    diagonal(s - 2).then_inc(step_done, 1)
                    n += 1
                v.wait_ge(step_done, ready)
                if s == 0:
                    nc.vector.tensor_tensor_scan(R[:, 1, 1:W + 1], M[:, 0, 1:W + 1], Dm[:, 0, 1:W + 1], init0[:, :],
                                                 ALU.min, ALU.add).then_inc(step_done, 1)
                else:
                    nc.vector.tensor_tensor_scan(R[:, s + 1, :], M[:, s, :], Dm[:, s, :], carry[:, s:s + 1],
                                                 ALU.min, ALU.add).then_inc(step_done, 1)
                n += 1
                scan_at.append(n)
                if s >= 2:
                    go_left(s - 2).then_inc(step_done, 1)
                    n += 1
            v.wait_ge(step_done, n)
            for s in (SLOTS - 2, SLOTS - 1):
                diagonal(s).then_inc(step_done, 1)
                go_left(s).then_inc(step_done, 1)
                n += 2
            v.wait_ge(step_done, n)

            def take_diagonal(s):
                return nc.vector.tensor_tensor(UD[:, s, :, 1], A[:, s, :], LC[:, s, :, 1], ALU.is_gt)

            def take_up(s):
                return nc.vector.scalar_tensor_tensor(out=UD[:, s, :, 0], in0=A[:, s, :], scalar=-1.0,
                                                      in1=LC[:, s, :, 1], op0=ALU.mult, op1=ALU.is_ge)

            take_diagonal(SLOTS - 1).then_inc(back_done, 1)
            take_up(SLOTS - 1).then_inc(back_done, 1)
            n = 2
            scan_n = 0
            for s in range(SLOTS - 1, -1, -1):
                if s < SLOTS - 1:
                    v.wait_ge(back_done, scan_n)
                    nc.vector.tensor_tensor(enter[:, s % 2, :, :],
                                            BK[:, s + 1, :, 0:1].to_broadcast([P, W, 2]), UD[:, s + 1, :, :],
                                            ALU.mult).then_inc(back_done, 1)
                    nc.vector.stream_shuffle(bcarry[:, s + 1:s + 2], BK[:, s + 1, W - 1, 1:2], left).then_inc(back_done, 1)
                    n += 2
                ready = n
                if s:
                    take_up(s - 1).then_inc(back_done, 1)
                    n += 1
                v.wait_ge(back_done, ready)
                nc.vector.tensor_tensor_scan(BK[:, s, :, :].rearrange("p w t -> p (w t)"),
                                             LC[:, s, :, :].rearrange("p w t -> p (w t)"),
                                             enter[:, s % 2, :, :].rearrange("p w t -> p (w t)"),
                                             bcarry[:, s + 1:s + 2], ALU.mult, ALU.add).then_inc(back_done, 1)
                n += 1
                scan_n = n
                if s:
                    take_diagonal(s - 1).then_inc(back_done, 1)
                    n += 1
                    scan_n = n
            v.wait_ge(back_done, n)
            nc.vector.transpose(PT[:, :, :], BK[:, :, :, 0]).then_inc(path_ready, 1)

            def before(g):
                c0 = chunk_of(g)
                gs = slice(4 * g, 4 * g + 4)
                for h in range(2):
                    v.wait_ge(aligned, 2 * g + h + 1)
                    xv = X[:, CH * h + c0:CH * h + c0 + 2, :]
                    nc.vector.tensor_tensor(xv, bank23[h][:, :, :], xv, ALU.add).then_inc(x1_ready, 1)
                for h in range(2):
                    v.wait_ge(x1_ready, 2 * g + h + 1)
                    for j in range(2):
                        nc.vector.bn_stats(stats2[:, 4 * g + 2 * h + j, :], X[:, CH * h + c0 + j, :]).then_inc(dve, 1)
                own[0] += 4
                v.wait_ge(dve, own[0])
                for t in range(4):
                    nc.vector.bn_aggr(mv2[:, 4 * g + t, :], stats2[:, 4 * g + t, :]).then_inc(dve, 1)
                own[0] += 4
                v.wait_ge(dve, own[0])
                nc.vector.tensor_scalar(rs16[:, gs], mv2[:, gs, 1], EPS, 1.0 / (ACT_ONE * ACT_ONE), ALU.add,
                                        ALU.mult).then_inc(var2_ready, 1)
                v.wait_ge(std2_ready, g + 1)
                link(nc.vector.reciprocal(rstd2[:, gs], std2[:, gs]))
                for h in range(2):
                    for j in range(2):
                        t = 2 * h + j
                        nc.vector.tensor_scalar(xq_int[:, g % 2, t, :], X[:, CH * h + c0 + j, :],
                                                mv2[:, 4 * g + t, 0:1], rstd2[:, 4 * g + t:4 * g + t + 1],
                                                ALU.subtract, ALU.mult).then_inc(dve, 1)
                own[0] += 4
                v.wait_ge(dve, own[0])
                if g >= 2:
                    v.wait_ge(xqT_done, g - 1)
                nc.vector.tensor_scalar(xq[:, g % 2, :, :], xq_int[:, g % 2, :, :], QMIN, QMAX, ALU.max,
                                        ALU.min).then_inc(quant_read, 1)

            def clip_hidden(g):
                for n in range(NH):
                    v.wait_ge(h_rounded, NH * g + n + 1)
                    if g >= 2 and n == 0:
                        v.wait_ge(y_done, 2 * (g - 1))
                    nc.vector.tensor_scalar(hq[:, g % 2, n, :], h_int[:, g % 2, n, :], 0.0, QMAX, ALU.max,
                                            ALU.min).then_inc(hq_ready, 1)

            def finish(g):
                c0 = chunk_of(g)
                for h in range(2):
                    v.wait_ge(y_done, 2 * g + h + 1)
                    v.wait_ge(biased, 2 * g + h + 1)
                    if g >= 2:
                        v.wait_ge(out_stored[g % 2][h], 16 * NQ * (g // 2))
                    nc.vector.scalar_tensor_tensor(
                        out=res[:, g % 2, 2 * h:2 * h + 2, :].rearrange("p j d -> p (j d)"),
                        in0=bank67[h][:, :, :].rearrange("p j d -> p (j d)"), scalar=1.0 / (ACT_ONE * W_ONE),
                        in1=X[:, CH * h + c0:CH * h + c0 + 2, :].rearrange("p j d -> p (j d)"),
                        op0=ALU.mult, op1=ALU.add).then_inc(res_ready, 1)

            before(0)
            before(1)
            clip_hidden(0)
            for g in range(NG):
                if g + 2 < NG:
                    before(g + 2)
                if g + 1 < NG:
                    clip_hidden(g + 1)
                finish(g)

        @block.tensor
        def _(pe):
            pe.wait_ge(ident_made, 2)
            pe.wait_ge(ctx_loaded, 16)
            for b in range(2):
                for m in range(4):
                    q, k = 2 * b + m // KH, m % KH
                    mm = nc.tensor.transpose(bank01[b][:, m * P:m * P + P], S[:, q, k * P:k * P + P], ident[:, :])
                mm.then_inc(ctxT_done, 1)
            pe.wait_ge(pool_const, 1)
            pe.wait_ge(ctx_sq, 2)
            for q in range(NQ):
                for k in range(KH):
                    mm = nc.tensor.matmul(bank5[W * q:W * q + W, 0:P], ones[:, :], ST2[:, q, k, :],
                                          start=(k == 0), stop=(k == KH - 1))
            mm.then_inc(aa_done, 1)

            def dots(k):
                h, c0, u0 = load_of(k)
                pe.wait_ge(xT_copied, (UL // 2) * (k + 1))
                flat = dist_banks[k][:, :, :].rearrange("p a b -> p (a b)")
                for j in range(UL):
                    for kk in range(KH):
                        for q in range(NQ):
                            mm = nc.tensor.matmul(flat[W * q:W * q + W, j * I:j * I + I],
                                                  XnT[:, k % 2, j, kk, W * q:W * q + W],
                                                  ST[:, q, kk, I * h:I * h + I], start=(kk == 0), stop=(kk == KH - 1))
                mm.then_inc(dot_done, 1)

            for k in range(LOADS):
                for j in range(UL // 2):
                    n = k * (UL // 2) + j
                    pe.wait_ge(xn_ready, UL * k + 2 * j + 2)
                    if n >= 2:
                        pe.wait_ge(xT_copied, n - 1)
                    for m in range(4):
                        mm = nc.tensor.transpose(bank01[n % 2][:, m * P:m * P + P],
                                                 Xn[:, k % 2, 2 * j + m // KH, (m % KH) * P:(m % KH) * P + P], ident[:, :])
                    mm.then_inc(xT_done, 1)
                if k >= 1:
                    dots(k - 1)
            dots(LOADS - 1)

            pe.wait_ge(pool_const, 7)
            pe.wait_ge(w_clip, 2)
            for n in range(NH):
                if n >= 2:
                    pe.wait_ge(wT_copied, n - 1)
                for m in range(4):
                    if n < NH // 2:
                        src = w1_q[:, 2 * n + m // KH, (m % KH) * P:(m % KH) * P + P]
                    else:
                        hh = 2 * (n - NH // 2) + m // OT
                        src = w2_q[:, m % OT, hh::NH]
                    mm = nc.tensor.transpose((flat4, path_ps)[n % 2][:, m * P:m * P + P], src, ident_bf[:, :])
                mm.then_inc(wT_done, 1)

            def align(g):
                c0 = chunk_of(g)
                if g >= 1:
                    pe.wait_ge(path_copied, g)
                for j in range(2):
                    c = c0 + j
                    for h in range(2):
                        mm = nc.tensor.transpose(path_ps[I * h:I * h + I, j * P:j * P + P],
                                                 PT[:, c:c + I, CH * h + c], flip[:, :])
                mm.then_inc(pathT_done, 1)
                pe.wait_ge(path_copied, g + 1)
                if g >= 1:
                    pe.wait_ge(x1_ready, 2 * g)
                for h in range(2):
                    for j in range(2):
                        for m, part in enumerate((S_hi, S_mid, S_lo)):
                            for q in range(NQ):
                                mm = nc.tensor.matmul(bank23[h][W * q:W * q + W, j, :],
                                                      PB[I * h:I * h + I, g % 2, j, W * q:W * q + W],
                                                      part[I * h:I * h + I, q, :], start=(m == 0), stop=(m == 2))
                    mm.then_inc(aligned, 1)

            def tokens_T(g):
                pe.wait_ge(quant_read, g + 1)
                if g >= 1:
                    pe.wait_ge(xqT_copied, g)
                for t in range(4):
                    for k in range(KH):
                        mm = nc.tensor.transpose(bank4[:, k, t * P:t * P + P], xq[:, g % 2, t, k * P:k * P + P],
                                                 ident_bf[:, :])
                mm.then_inc(xqT_done, 1)

            def hidden(g):
                pe.wait_ge(xqT_copied, g + 1)
                for n in range(NH):
                    if NH * g + n >= 2:
                        pe.wait_ge(h_rounded, NH * g + n - 1)
                    for k in range(KH):
                        mm = nc.tensor.matmul(bank01[n % 2][:, :], w1T[:, k, n * P:n * P + P], xqT[:, g % 2, k, :],
                                              start=(k == 0), stop=(k == KH - 1))
                    mm.then_inc(h_done, 1)

            def output(g):
                if g >= 1:
                    pe.wait_ge(res_ready, 2 * g)
                pe.wait_ge(hq_ready, NH * (g + 1))
                for h in range(2):
                    for j in range(2):
                        t = 2 * h + j
                        for n in range(NH):
                            mm = nc.tensor.matmul(bank67[h][:, j, :], hq[:, g % 2, n, t * P:t * P + P], w2T[:, n, :],
                                                  start=(n == 0), stop=(n == NH - 1))
                    mm.then_inc(y_done, 1)

            pe.wait_ge(path_ready, 1)
            pe.wait_ge(ctx_split, 4)
            pe.wait_ge(pool_const, 8)
            pe.wait_ge(wT_copied, NH)
            align(0)
            align(1)
            tokens_T(0)
            hidden(0)
            for g in range(NG):
                if g + 2 < NG:
                    align(g + 2)
                if g + 1 < NG:
                    tokens_T(g + 1)
                    hidden(g + 1)
                output(g)


_INS = ['x', 'ctx_1024', 'L0_ffn_w1', 'L0_ffn_b1', 'L0_ffn_w2', 'L0_ffn_b2']


def kernel(**inputs):
    import numpy as _np
    import concourse.bacc as _bacc
    from concourse import mybir as _mybir
    from concourse.bass_utils import run_bass_kernel_spmd as _run

    nc = _bacc.Bacc("TRN2", target_bir_lowering=False, num_devices=1)
    arrays, args = {}, []
    for name in _INS:
        a = _np.ascontiguousarray(inputs[name])
        arrays[f"in_{name}_dram"] = a
        args.append(nc.dram_tensor(f"in_{name}_dram", a.shape, _mybir.dt.from_np(a.dtype), kind="ExternalInput").ap())
    args.append(nc.dram_tensor("out_dram", (B, T, D), _mybir.dt.float32, kind="ExternalOutput").ap())
    align_ffn_kernel(nc, *args)
    r = _run(nc, [arrays], core_ids=[0])
    return r.results[0]["out_dram"]
```

```python
import concourse.bass as bass
from concourse import mybir
from contextlib import ExitStack

BIG = 1e30
B, T, D = 8, 512, 256
I = 64
HID = 1024
P = 128
W = 32
CH = T // W
NQ = P // W
NU = 2 * CH
SLOTS = I + CH - 1
KH = D // P
EPS = 1e-5
LOADS = 4
CL = CH // LOADS
UL = 2 * CL
NG = NU // 4
HEAD = CH - 2
PIECE = 13
PIECES = (SLOTS - HEAD) // PIECE
NR = NQ * D // I
assert PIECES * PIECE == SLOTS - HEAD
NH = HID // P
OT = D // P
ACT_ONE, W_ONE = 16.0, 64.0
QMAX, QMIN = 127.0, -128.0


def align_ffn_kernel(nc: bass.Bass, x, ctx_in, w1, b1, w2, b2, out):
    f32, bf16, i16 = mybir.dt.float32, mybir.dt.bfloat16, mybir.dt.int16
    ALU, ACT = mybir.AluOpType, mybir.ActivationFunctionType

    x_v = x.rearrange("(q h) (c w) d -> q h w c d", h=2, w=W)
    out_v = out.rearrange("(q h) (c w) d -> q h w c d", h=2, w=W)
    ctx_v = ctx_in.rearrange("(q h) i d -> (h i) q d", h=2)

    with ExitStack() as ctx:
        def sb(name, shape, dt=f32):
            return ctx.enter_context(nc.sbuf_tensor(name, shape, dt))

        def bank(name, shape, dt=f32):
            return ctx.enter_context(nc.psum_tensor(name, shape, dt))

        def sem(name):
            return ctx.enter_context(nc.semaphore(name))

        X = sb("X", [P, NU, D])
        Xn = sb("Xn", [P, 2, UL, D])
        XnT = sb("XnT", [P, 2, UL, KH, P])
        stats = sb("stats", [P, NU, 6])
        mv = sb("mv", [P, NU, 2])
        std = sb("std", [P, NU])
        rstd = sb("rstd", [P, NU])
        vr = sb("vr", [P, NU])
        bb = sb("bb", [P, NU])
        S = sb("S", [P, NQ, D])
        S_hi = sb("S_hi", [P, NQ, D], bf16)
        S_hm = sb("S_hm", [P, 2, NQ, D], bf16)
        S_mid = sb("S_mid", [P, NQ, D], bf16)
        S_lo = sb("S_lo", [P, NQ, D], bf16)
        ST = sb("ST", [P, NQ, KH, P])
        ST2 = sb("ST2", [P, NQ, KH, P])
        S_r1 = ST2[:, :, :, :].rearrange("p q k n -> p q (k n)")
        aa = sb("aa", [P, 2, I])
        norms = sb("norms", [P, LOADS, UL, I])
        E = sb("E", [P, SLOTS, NU])
        Dm = sb("Dm", [P, SLOTS, W + 1])
        M = sb("M", [P, SLOTS, W + 1])
        R = sb("R", [P, SLOTS + 1, W + 1])
        carry = sb("carry", [P, SLOTS + 1])
        init0 = sb("init0", [P, 1])
        NL = sb("NL", [P, SLOTS, W + 1], bf16)
        A = sb("A", [P, SLOTS, W], bf16)
        code = sb("code", [P, SLOTS, W], bf16)
        Y = sb("Y", [P, SLOTS, W + 1], bf16)
        enter = sb("enter", [P, 2, W + 1], bf16)
        bcarry = sb("bcarry", [P, SLOTS + 1], bf16)
        PT = sb("PT", [P, SLOTS, NU], bf16)
        chunk0 = sb("chunk0", [P, B])
        chunk15 = sb("chunk15", [P, B])
        first = sb("first", [P, 1])
        last = sb("last", [P, 1])
        ident = sb("ident", [P, P])
        ident_bf = sb("ident_bf", [P, P], bf16)
        flip = sb("flip", [P, P], bf16)
        ones = sb("ones", [P, W])
        w1_raw = sb("w1_raw", [P, NH, D])
        w2_raw = sb("w2_raw", [P, OT, HID])
        w_int = sb("w_int", [P, 2, NH * D], i16)
        w1_q = w1_raw[:, :, :].rearrange("p n d -> p (n d)").bitcast(bf16)[:, 0:NH * D].rearrange(
            "p (n d) -> p n d", d=D)
        w2_q = w2_raw[:, :, :].rearrange("p n d -> p (n d)").bitcast(bf16)[:, 0:OT * HID].rearrange(
            "p (n d) -> p n d", d=HID)
        w1T = sb("w1T", [P, KH, HID], bf16)
        w2T = sb("w2T", [P, NH, D], bf16)
        b1_raw = sb("b1_raw", [P, NH])
        b1_int = sb("b1_int", [P, NH], i16)
        b1_q = sb("b1_q", [P, NH])
        b1_s = sb("b1_s", [P, NH])
        b2_raw = sb("b2_raw", [P, D])
        b2_int = sb("b2_int", [P, D], i16)
        b2_q = sb("b2_q", [P, D])
        b2_s = sb("b2_s", [P, D])
        PB = sb("PB", [P, 2, 2, 2, P], bf16)
        stats2 = sb("stats2", [P, NU, 6])
        mv2 = sb("mv2", [P, NU, 2])
        std2 = sb("std2", [P, NU])
        rstd2 = sb("rstd2", [P, NU])
        rs16 = sb("rs16", [P, NU])
        xq_both = Dm[:, :, :].rearrange("p s w -> p (s w)")[:, 0:4 * D * 2]
        xq_int = xq_both[:, 0:4 * D].bitcast(i16).rearrange("p (a t d) -> p a t d", a=2, t=4)
        xq = xq_both[:, 4 * D:8 * D].bitcast(bf16).rearrange("p (a t d) -> p a t d", a=2, t=4)
        xqT = M[:, :, :].rearrange("p s w -> p (s w)")[:, 0:KH * 4 * P].bitcast(bf16).rearrange(
            "p (a k n) -> p a k n", a=2, k=KH)
        h_int = Xn[:, :, :, :].rearrange("p a u d -> p (a u d)").bitcast(i16).rearrange(
            "p (a n t) -> p a n t", a=2, n=NH)
        hq = XnT[:, :, :, :, :].rearrange("p a u k d -> p (a u k d)").bitcast(bf16).rearrange(
            "p (a n t) -> p a n t", a=2, n=NH)
        res = E[:, :, :].rearrange("p s u -> p (s u)")[:, 0:8 * D].rearrange("p (a t d) -> p a t d", a=2, t=4)

        bank01 = [bank("h0", [P, 512]), bank("h1", [P, 512])]
        bank23 = [bank("e0", [P, 2, D]), bank("e1", [P, 2, D])]
        bank4 = bank("t4", [P, 2, 4 * P], bf16)
        bank5 = bank("t5", [P, 512])
        bank67 = [bank("y0", [P, 2, D]), bank("y1", [P, 2, D])]
        path_ps = bank5[:, :].bitcast(bf16)
        flat4 = bank4[:, :, :].rearrange("p a b -> p (a b)")

        x_in = [sem(f"x_in{k}") for k in range(LOADS)]
        ctx_loaded = sem("ctx_loaded")
        w_loaded = sem("w_loaded")
        out_stored = [[sem(f"out_stored{a}{h}") for h in range(2)] for a in range(2)]
        ident_made = sem("ident_made")
        pool_const = sem("pool_const")
        norms_made = sem("norms_made")
        skewed = sem("skewed")
        clamped = sem("clamped")
        ctx_split = sem("ctx_split")
        ctx_rest = sem("ctx_rest")
        ctx_stacked = sem("ctx_stacked")
        w_clip = sem("w_clip")
        b_clip = sem("b_clip")
        biased = sem("biased")
        dve = sem("dve")
        var_ready = sem("var_ready")
        bb_ready = sem("bb_ready")
        xn_ready = sem("xn_ready")
        dist2_ready = sem("dist2_ready")
        step_done = sem("step_done")
        back_done = sem("back_done")
        cells_done = sem("cells_done")
        path_ready = sem("path_ready")
        x1_ready = sem("x1_ready")
        var2_ready = sem("var2_ready")
        quant_read = sem("quant_read")
        xq_ready = sem("xq_ready")
        hq_ready = sem("hq_ready")
        res_ready = sem("res_ready")
        std_ready = sem("std_ready")
        ctxT_copied = sem("ctxT_copied")
        ctx_sq = sem("ctx_sq")
        aa_copied = sem("aa_copied")
        xT_copied = sem("xT_copied")
        rooted = sem("rooted")
        w_rounded = sem("w_rounded")
        wT_copied = sem("wT_copied")
        path_copied = sem("path_copied")
        std2_ready = sem("std2_ready")
        xqT_copied = sem("xqT_copied")
        h_rounded = sem("h_rounded")
        ctxT_done = sem("ctxT_done")
        aa_done = sem("aa_done")
        xT_done = sem("xT_done")
        dot_done = sem("dot_done")
        wT_done = sem("wT_done")
        pathT_done = sem("pathT_done")
        aligned = sem("aligned")
        xqT_done = sem("xqT_done")
        h_done = sem("h_done")
        y_done = sem("y_done")


        def tile_of(k, j):
            return CH * (j // CL) + CL * k + j % CL

        def by_half(ap):
            return ap.rearrange("p (h c) i -> p h c i", h=2)

        def chunk_of(g):
            return CH - 2 - 2 * g

        dist_banks = [bank23[0], bank23[1], bank67[0], bank67[1]]

        block = ctx.enter_context(nc.Block())

        @block.sync
        def _(sp):
            sp.dma_start(S[:, :, :], ctx_v).then_inc(ctx_loaded, 16)
            for k in range(LOADS):
                for h in range(2):
                    u0 = tile_of(k, CL * h)
                    for q in range(NQ):
                        sp.dma_start(X[W * q:W * q + W, u0:u0 + CL, :],
                                     x_v[q, h, :, CL * k:CL * k + CL, :]).then_inc(x_in[k], 16)
            sp.dma_start(w1_raw[:, :, :], w1.rearrange("(p n) d -> p n d", n=NH)).then_inc(w_loaded, 16)
            sp.dma_start(w2_raw[:, :, :], w2.rearrange("(n p) d -> p n d", p=P)).then_inc(w_loaded, 16)
            sp.dma_start(b2_raw[:, :], b2.partition_broadcast(P)).then_inc(w_loaded, 16)
            sp.dma_start(b1_raw[:, :], b1.rearrange("(p n) -> p n", n=NH)).then_inc(w_loaded, 16)
            sp.wait_ge(ctx_split, 2)
            for part, turned in ((S_hi, 0), (S_mid, 1)):
                for h in range(2):
                    at = I * (h ^ turned)
                    sp.dma_start(S_hm[at:at + I, h, :, :], part[I * h:I * h + I, :, :]).then_inc(ctx_stacked, 16)
            for g in range(NG):
                c0 = chunk_of(g)
                for h in range(2):
                    sp.wait_ge(res_ready, 2 * g + h + 1)
                    for q in range(NQ):
                        sp.dma_start(out_v[q, h, :, c0:c0 + 2, :],
                                     res[W * q:W * q + W, g % 2, 2 * h:2 * h + 2, :]).then_inc(out_stored[g % 2][h], 16)
            for a in range(2):
                for h in range(2):
                    sp.wait_ge(out_stored[a][h], 16 * NQ * (NG // 2))

        @block.gpsimd
        def _(pool):
            nc.gpsimd.memset(ident[:, :], 0.0).then_inc(ident_made, 1)
            pool.wait_ge(ident_made, 1)
            nc.gpsimd.affine_select(out=ident[:, :], in_=ident[:, :], compare_op=ALU.not_equal, fill=1.0, base=0,
                                    pattern=[[-1, P]], channel_multiplier=1).then_inc(ident_made, 1)
            nc.gpsimd.memset(ones[:, :], 1.0).then_inc(pool_const, 1)
            nc.gpsimd.memset(ident_bf[:, :], 0.0).then_inc(pool_const, 1)
            nc.gpsimd.memset(flip[:, :], 0.0).then_inc(pool_const, 1)
            nc.gpsimd.memset(chunk0[:, :], 0.0).then_inc(pool_const, 1)
            nc.gpsimd.memset(chunk15[:, :], 0.0).then_inc(pool_const, 1)
            nc.gpsimd.memset(E[:, :, :], 0.0).then_inc(pool_const, 1)
            pool.wait_ge(pool_const, 6)
            nc.gpsimd.affine_select(out=ident_bf[:, :], in_=ident_bf[:, :], compare_op=ALU.not_equal, fill=1.0,
                                    base=0, pattern=[[-1, P]], channel_multiplier=1).then_inc(pool_const, 1)
            nc.gpsimd.affine_select(out=flip[:, :].rearrange("p (a b) -> p a b", b=W),
                                    in_=flip[:, :].rearrange("p (a b) -> p a b", b=W),
                                    compare_op=ALU.not_equal, fill=1.0, base=-(W - 1),
                                    pattern=[[-W, NQ], [1, W]], channel_multiplier=1).then_inc(pool_const, 1)
            for t, off in ((chunk0, 0), (chunk15, CH - 1)):
                nc.gpsimd.affine_select(out=t[:, :], in_=t[:, :], compare_op=ALU.not_equal, fill=1.0, base=-off,
                                        pattern=[[-CH, B]], channel_multiplier=1).then_inc(pool_const, 1)
            nc.gpsimd.memset(Dm[:, 0, 0:1], 0.0).then_inc(pool_const, 1)
            nc.gpsimd.memset(Dm[:, 1:SLOTS, 0:1], 0.0).then_inc(pool_const, 1)
            nc.gpsimd.memset(M[:, :, 0:1], BIG).then_inc(pool_const, 1)
            nc.gpsimd.memset(R[:, 0, :], BIG).then_inc(pool_const, 1)
            nc.gpsimd.memset(R[:, 1, 0:1], BIG).then_inc(pool_const, 1)
            nc.gpsimd.memset(NL[:, :, 0:1], 0.0).then_inc(pool_const, 1)
            nc.gpsimd.memset(enter[:, :, :], 0.0).then_inc(pool_const, 1)

            pool.wait_ge(aa_copied, 1)
            for k in range(LOADS):
                pool.wait_ge(bb_ready, k + 1)
                nc.gpsimd.tensor_tensor(by_half(norms[:, k, :, :]), aa[:, :, :].unsqueeze(2).to_broadcast([P, 2, CL, I]),
                                        by_half(bb[:, UL * k:UL * k + UL].unsqueeze(2)).to_broadcast([P, 2, CL, I]),
                                        ALU.add).then_inc(norms_made, 1)

            pool.wait_ge(w_rounded, 4)
            nc.gpsimd.tensor_scalar(b1_q[:, :], b1_int[:, :], QMAX, QMIN, ALU.min, ALU.max).then_inc(b_clip, 1)
            nc.gpsimd.tensor_scalar(b2_q[:, :], b2_int[:, :], QMAX, QMIN, ALU.min, ALU.max).then_inc(b_clip, 1)
            pool.wait_ge(b_clip, 2)
            nc.gpsimd.tensor_scalar(b1_s[:, :], b1_q[:, :], ACT_ONE / W_ONE, 0.0, ALU.mult, ALU.add).then_inc(b_clip, 1)
            nc.gpsimd.tensor_scalar(b2_s[:, :], b2_q[:, :], 1.0 / W_ONE, 0.0, ALU.mult, ALU.add).then_inc(b_clip, 1)
            pool.wait_ge(b_clip, 4)

            for g in range(NG):
                c0 = chunk_of(g)
                pool.wait_ge(quant_read, g + 1)
                for h in range(2):
                    v = X[:, CH * h + c0:CH * h + c0 + 2, :]
                    nc.gpsimd.tensor_tensor(v, v, b2_s[:, :].unsqueeze(1).to_broadcast([P, 2, D]),
                                            ALU.add).then_inc(biased, 1)

        @block.scalar
        def _(act):
            for b in range(2):
                act.wait_ge(ctxT_done, b + 1)
                nc.scalar.activation(ST[:, 2 * b:2 * b + 2, :, :].rearrange("p q k n -> p (q k n)"), bank01[b][:, :],
                                     ACT.Copy).then_inc(ctxT_copied, 1)
                act.wait_ge(ctxT_copied, b + 1)
                nc.scalar.activation(ST2[:, 2 * b:2 * b + 2, :, :], ST[:, 2 * b:2 * b + 2, :, :],
                                     ACT.Square).then_inc(ctx_sq, 1)
            act.wait_ge(aa_done, 1)
            nc.scalar.activation(aa[:, :, :].rearrange("p h i -> p (h i)"), bank5[:, 0:P], ACT.Copy).then_inc(aa_copied, 1)

            def roots(k):
                act.wait_ge(dist2_ready, k + 1)
                nc.scalar.activation(norms[:, k, :, :], norms[:, k, :, :], ACT.Relu).then_inc(clamped, 1)
                act.wait_ge(clamped, k + 1)
                act.wait_ge(pool_const, 6)
                c0 = CL * k
                dst = bass.AP(E, c0 * NU + c0, [[SLOTS * NU, P], [CH, 2], [NU + 1, CL], [NU, I]])
                nc.scalar.activation(dst, by_half(norms[:, k, :, :]), ACT.Sqrt).then_inc(rooted, 1)

            def spread(k):
                act.wait_ge(var_ready, k + 1)
                nc.scalar.activation(std[:, UL * k:UL * k + UL], vr[:, UL * k:UL * k + UL], ACT.Sqrt).then_inc(std_ready, 1)

            spread(0)
            for k in range(LOADS):
                if k + 1 < LOADS:
                    spread(k + 1)
                for j in range(UL // 2):
                    n = k * (UL // 2) + j
                    act.wait_ge(xT_done, n + 1)
                    if k >= 2 and j == 0:
                        act.wait_ge(dot_done, k - 1)
                    nc.scalar.activation(XnT[:, k % 2, 2 * j:2 * j + 2, :, :].rearrange("p u k n -> p (u k n)"),
                                         bank01[n % 2][:, :], ACT.Copy).then_inc(xT_copied, 1)
                if k >= 1:
                    roots(k - 1)
            roots(LOADS - 1)

            nc.scalar.activation(S_hi[:, :, :], S[:, :, :], ACT.Copy).then_inc(ctx_split, 1)
            act.wait_ge(w_loaded, 64)
            nc.scalar.activation(w_int[:, 0, :], w1_raw[:, :, :].rearrange("p n d -> p (n d)"), ACT.Copy,
                                 scale=W_ONE).then_inc(w_rounded, 1)
            nc.scalar.activation(w_int[:, 1, :], w2_raw[:, :, :].rearrange("p n d -> p (n d)"), ACT.Copy,
                                 scale=W_ONE).then_inc(w_rounded, 1)
            nc.scalar.activation(b1_int[:, :], b1_raw[:, :], ACT.Copy, scale=W_ONE).then_inc(w_rounded, 1)
            nc.scalar.activation(b2_int[:, :], b2_raw[:, :], ACT.Copy, scale=W_ONE).then_inc(w_rounded, 1)
            act.wait_ge(ctx_rest, NR)
            nc.scalar.activation(S_mid[:, :, :], S_r1[:, :, :], ACT.Copy).then_inc(ctx_split, 1)
            for n in range(NH):
                act.wait_ge(wT_done, n + 1)
                src = (flat4, path_ps)[n % 2][:, 0:512]
                if n < NH // 2:
                    dst = w1T[:, :, 2 * n * P:2 * n * P + 2 * P].rearrange("p k (m n) -> p m k n", m=2)
                    src = src.rearrange("p (m k n) -> p m k n", m=2, k=KH)
                else:
                    m = n - NH // 2
                    dst = w2T[:, 2 * m:2 * m + 2, :].rearrange("p m n -> p (m n)")
                nc.scalar.activation(dst, src, ACT.Copy).then_inc(wT_copied, 1)

            def copy_path(g):
                act.wait_ge(pathT_done, g + 1)
                if g >= 2:
                    act.wait_ge(aligned, 2 * (g - 1))
                nc.scalar.activation(PB[:, g % 2, :, :, :].rearrange("p j h n -> p (j h n)"), path_ps[:, 0:4 * P],
                                     ACT.Copy).then_inc(path_copied, 1)

            def deviation(g):
                act.wait_ge(var2_ready, g + 1)
                nc.scalar.activation(std2[:, 4 * g:4 * g + 4], rs16[:, 4 * g:4 * g + 4], ACT.Sqrt).then_inc(std2_ready, 1)

            def copy_xqT(g):
                act.wait_ge(xqT_done, g + 1)
                if g >= 2:
                    act.wait_ge(h_done, NH * (g - 1))
                nc.scalar.activation(xqT[:, g % 2, :, :], bank4[:, :, :], ACT.Copy).then_inc(xqT_copied, 1)

            def round_hidden(g, n):
                act.wait_ge(h_done, NH * g + n + 1)
                if g >= 2 and n == 0:
                    act.wait_ge(hq_ready, NH * (g - 1))
                nc.scalar.activation(h_int[:, g % 2, n, :], bank01[n % 2][:, :], ACT.Identity, bias=b1_s[:, n:n + 1],
                                     scale=1.0 / W_ONE).then_inc(h_rounded, 1)

            copy_path(0)
            copy_path(1)
            deviation(0)
            act.wait_ge(b_clip, 4)
            copy_xqT(0)
            copy_path(2)
            for n in range(NH):
                round_hidden(0, n)
                if n == 3:
                    deviation(1)
                if n == 6:
                    copy_xqT(1)
            for g in range(NG - 1):
                for n in range(NH):
                    round_hidden(g + 1, n)
                    if g + 3 < NG and n == 1:
                        copy_path(g + 3)
                    if g + 2 < NG:
                        if n == 3:
                            deviation(g + 2)
                        if n == 6:
                            copy_xqT(g + 2)

        @block.vector
        def _(v):
            own = [0]

            def link(ins):
                own[0] += 1
                ins.then_inc(dve, 1)
                v.wait_ge(dve, own[0])

            v.wait_ge(pool_const, 17)
            nc.vector.reduce_max(first[:, :], chunk0[:, :], mybir.AxisListType.X).then_inc(dve, 1)
            nc.vector.reduce_max(last[:, :], chunk15[:, :], mybir.AxisListType.X).then_inc(dve, 1)
            own[0] += 2
            v.wait_ge(dve, own[0])
            nc.vector.tensor_scalar(init0[:, :], first[:, :], -BIG, BIG, ALU.mult, ALU.add).then_inc(dve, 1)
            nc.vector.tensor_scalar(Dm[:, 1:SLOTS, 0], Dm[:, 1:SLOTS, 0], 1.0, first[:, :], ALU.mult,
                                    ALU.add).then_inc(dve, 1)
            nc.vector.tensor_copy(bcarry[:, SLOTS:SLOTS + 1], last[:, :]).then_inc(dve, 1)
            own[0] += 3
            v.wait_ge(dve, own[0])
            link(nc.vector.tensor_scalar(Dm[:, 1:SLOTS, 0], Dm[:, 1:SLOTS, 0], BIG, None, ALU.mult))

            def distances(k):
                v.wait_ge(dot_done, k + 1)
                v.wait_ge(norms_made, k + 1)
                nc.vector.scalar_tensor_tensor(out=norms[:, k, :, :].rearrange("p u i -> p (u i)"),
                                               in0=dist_banks[k][:, :, :].rearrange("p a b -> p (a b)"), scalar=-2.0,
                                               in1=norms[:, k, :, :].rearrange("p u i -> p (u i)"),
                                               op0=ALU.mult, op1=ALU.add).then_inc(dist2_ready, 1)

            def statistics(k):
                us = range(UL * k, UL * k + UL)
                v.wait_ge(x_in[k], 16 * 2 * NQ)
                for u in us:
                    nc.vector.bn_stats(stats[:, u, :], X[:, tile_of(k, u - UL * k), :]).then_inc(dve, 1)
                own[0] += UL
                v.wait_ge(dve, own[0])
                for u in us:
                    nc.vector.bn_aggr(mv[:, u, :], stats[:, u, :]).then_inc(dve, 1)
                own[0] += UL
                v.wait_ge(dve, own[0])
                nc.vector.tensor_scalar(vr[:, UL * k:UL * k + UL], mv[:, UL * k:UL * k + UL, 1], EPS, None,
                                        ALU.add).then_inc(var_ready, 1)

            def normalise(k):
                us = slice(UL * k, UL * k + UL)
                v.wait_ge(std_ready, k + 1)
                link(nc.vector.reciprocal(rstd[:, us], std[:, us]))
                link(nc.vector.tensor_tensor(bb[:, us], mv[:, us, 1], rstd[:, us], ALU.mult))
                if k >= 2:
                    v.wait_ge(xT_done, (UL // 2) * (k - 1))
                for j in range(UL):
                    u = UL * k + j
                    nc.vector.tensor_scalar(Xn[:, k % 2, j, :], X[:, tile_of(k, j), :], mv[:, u, 0:1],
                                            rstd[:, u:u + 1], ALU.subtract, ALU.mult).then_inc(xn_ready, 1)
                    if j == 0:
                        nc.vector.scalar_tensor_tensor(out=bb[:, us], in0=bb[:, us], scalar=float(D),
                                                       in1=rstd[:, us], op0=ALU.mult, op1=ALU.mult).then_inc(bb_ready, 1)

            def to_chunks(k):
                lo, hi = CL * k, (CL * k + CL if k + 1 < LOADS else SLOTS)
                v.wait_ge(rooted, k + 1)
                nc.vector.transpose(Dm[:, lo:hi, 1:W + 1], E[:, lo:hi, :]).then_inc(skewed, 1)

            right = [W - 1] + list(range(W - 1))
            left = list(range(1, W)) + [0]

            def not_left(s):
                return nc.vector.tensor_tensor(NL[:, s, 1:W + 1], M[:, s, W:0:-1], R[:, s + 1, W - 1::-1], ALU.is_le)

            def diagonal(s):
                return nc.vector.tensor_tensor(A[:, s, :], R[:, s, W - 1::-1], M[:, s, W:0:-1], ALU.is_le)

            steps = [0]
            scan_at = []

            def signal(ins):
                steps[0] += 1
                ins.then_inc(step_done, 1)

            def forward(lo, hi, loads):
                v.wait_ge(skewed, loads)
                for s in range(lo, hi):
                    if s:
                        v.wait_ge(step_done, scan_at[s - 1])
                    signal(nc.vector.tensor_tensor(M[:, s, 1:W + 1], R[:, s, 1:W + 1], R[:, s, 0:W], ALU.min))
                    if s:
                        signal(nc.vector.stream_shuffle(carry[:, s:s + 1], R[:, s, W:W + 1], right))
                    ready = steps[0]
                    if s >= 2:
                        signal(diagonal(s - 2))
                    v.wait_ge(step_done, ready)
                    if s == 0:
                        signal(nc.vector.tensor_tensor_scan(R[:, 1, 1:W + 1], M[:, 0, 1:W + 1], Dm[:, 0, 1:W + 1],
                                                            init0[:, :], ALU.min, ALU.add))
                    else:
                        signal(nc.vector.tensor_tensor_scan(R[:, s + 1, :], M[:, s, :], Dm[:, s, :],
                                                            carry[:, s:s + 1], ALU.min, ALU.add))
                    scan_at.append(steps[0])
                    if s >= 2:
                        signal(not_left(s - 2))

            statistics(0)
            statistics(1)
            normalise(0)
            statistics(2)
            normalise(1)
            distances(0)
            statistics(3)
            normalise(2)
            distances(1)
            normalise(3)
            to_chunks(0)
            forward(0, CL, 1)
            distances(2)
            to_chunks(1)
            forward(CL, 2 * CL, 2)
            distances(3)
            to_chunks(2)
            forward(2 * CL, 3 * CL, 3)
            to_chunks(3)
            forward(3 * CL, SLOTS, 4)
            v.wait_ge(step_done, steps[0])
            for s in (SLOTS - 2, SLOTS - 1):
                signal(diagonal(s))
                signal(not_left(s))
            v.wait_ge(step_done, steps[0])

            def steps_of(s):
                return nc.vector.scalar_tensor_tensor(out=code[:, s, :], in0=A[:, s, :], scalar=1.0,
                                                      in1=NL[:, s, 1:W + 1], op0=ALU.add, op1=ALU.mult)

            def on_path(lo, hi):
                nc.vector.tensor_scalar(A[:, lo:hi, :], Y[:, lo:hi, 0:W], 1.0, None, ALU.is_equal).then_inc(cells_done, 1)

            def path_tokens(lo, hi, count):
                v.wait_ge(cells_done, count)
                nc.vector.transpose(PT[:, lo:hi, :], A[:, lo:hi, :]).then_inc(path_ready, 1)

            S_f, S_hi_f, S_mid_f, S_lo_f = (t[:, :, :].rearrange("p q d -> p (q d)") for t in (S, S_hi, S_mid, S_lo))
            S_r1_f = S_r1.rearrange("p q d -> p (q d)")

            def split_piece(i):
                if i == 0:
                    v.wait_ge(ctx_split, 1)
                    v.wait_ge(aa_done, 1)
                at = slice(I * i, I * i + I)
                nc.vector.tensor_tensor(S_r1_f[:, at], S_f[:, at], S_hi_f[:, at], ALU.subtract).then_inc(ctx_rest, 1)

            def rest_piece(i):
                if i == 0:
                    v.wait_ge(ctx_split, 2)
                at = slice(I * i, I * i + I)
                nc.vector.tensor_tensor(S_lo_f[:, at], S_r1_f[:, at], S_mid_f[:, at], ALU.subtract).then_inc(ctx_rest, 1)

            def clip_piece(i):
                if i == 0:
                    v.wait_ge(w_rounded, 4)
                half, at = i // NH, slice(D * (i % NH), D * (i % NH) + D)
                dst = (w1_q, w2_q)[half].rearrange("p a b -> p (a b)")
                nc.vector.tensor_scalar(dst[:, at], w_int[:, half, at], QMAX, QMIN, ALU.min, ALU.max).then_inc(w_clip, 1)

            def add_aligned(g):
                c0 = chunk_of(g)
                for h in range(2):
                    v.wait_ge(aligned, 2 * g + h + 1)
                    xv = X[:, CH * h + c0:CH * h + c0 + 2, :]
                    nc.vector.tensor_tensor(xv, bank23[h][:, :, :], xv, ALU.add).then_inc(x1_ready, 1)
                for h in range(2):
                    v.wait_ge(x1_ready, 2 * g + h + 1)
                    for j in range(2):
                        nc.vector.bn_stats(stats2[:, 4 * g + 2 * h + j, :], X[:, CH * h + c0 + j, :]).then_inc(dve, 1)
                own[0] += 4
                v.wait_ge(dve, own[0])
                for t in range(4):
                    nc.vector.bn_aggr(mv2[:, 4 * g + t, :], stats2[:, 4 * g + t, :]).then_inc(dve, 1)
                own[0] += 4
                v.wait_ge(dve, own[0])
                nc.vector.tensor_scalar(rs16[:, 4 * g:4 * g + 4], mv2[:, 4 * g:4 * g + 4, 1], EPS,
                                        1.0 / (ACT_ONE * ACT_ONE), ALU.add, ALU.mult).then_inc(var2_ready, 1)

            def quantise(g):
                c0 = chunk_of(g)
                v.wait_ge(std2_ready, g + 1)
                link(nc.vector.reciprocal(rstd2[:, 4 * g:4 * g + 4], std2[:, 4 * g:4 * g + 4]))
                for h in range(2):
                    for j in range(2):
                        t = 2 * h + j
                        nc.vector.tensor_scalar(xq_int[:, g % 2, t, :], X[:, CH * h + c0 + j, :],
                                                mv2[:, 4 * g + t, 0:1], rstd2[:, 4 * g + t:4 * g + t + 1],
                                                ALU.subtract, ALU.mult).then_inc(dve, 1)
                own[0] += 4
                v.wait_ge(dve, own[0])
                if g >= 2:
                    v.wait_ge(xqT_done, g - 1)
                nc.vector.tensor_scalar(xq[:, g % 2, :, :], xq_int[:, g % 2, :, :], QMIN, QMAX, ALU.max,
                                        ALU.min).then_inc(quant_read, 1)

            def clip_hidden(g, n):
                v.wait_ge(h_rounded, NH * g + n + 1)
                if g >= 2 and n == 0:
                    v.wait_ge(y_done, 2 * (g - 1))
                nc.vector.tensor_scalar(hq[:, g % 2, n, :], h_int[:, g % 2, n, :], 0.0, QMAX, ALU.max,
                                        ALU.min).then_inc(hq_ready, 1)

            def finish(g, h):
                c0 = chunk_of(g)
                v.wait_ge(y_done, 2 * g + h + 1)
                v.wait_ge(biased, 2 * g + h + 1)
                if g >= 2:
                    v.wait_ge(out_stored[g % 2][h], 16 * NQ * (g // 2))
                nc.vector.scalar_tensor_tensor(
                    out=res[:, g % 2, 2 * h:2 * h + 2, :].rearrange("p j d -> p (j d)"),
                    in0=bank67[h][:, :, :].rearrange("p j d -> p (j d)"), scalar=1.0 / (ACT_ONE * W_ONE),
                    in1=X[:, CH * h + c0:CH * h + c0 + 2, :].rearrange("p j d -> p (j d)"),
                    op0=ALU.mult, op1=ALU.add).then_inc(res_ready, 1)

            steps_of(SLOTS - 1).then_inc(back_done, 1)
            n = 1
            scan_n = 0
            cells = 0
            for s in range(SLOTS - 1, -1, -1):
                if s < SLOTS - 1:
                    v.wait_ge(back_done, scan_n)
                    nc.vector.scalar_tensor_tensor(out=enter[:, s % 2, 0:W], in0=Y[:, s + 1, 0:W], scalar=1.0,
                                                   in1=code[:, s + 1, :], op0=ALU.is_equal,
                                                   op1=ALU.mult).then_inc(back_done, 1)
                    nc.vector.stream_shuffle(bcarry[:, s + 1:s + 2], Y[:, s + 1, W:W + 1], left).then_inc(back_done, 1)
                    n += 2
                    i = SLOTS - 2 - s
                    if i < NR:
                        split_piece(i)
                    elif NR + 4 <= i < 2 * NR + 4:
                        rest_piece(i - NR - 4)
                    elif 2 * NR + 4 <= i < 2 * NR + 4 + 2 * NH:
                        clip_piece(i - 2 * NR - 4)
                    lo = s + 1
                    if lo < HEAD and (HEAD - lo) % 2 == 0:
                        on_path(lo, lo + 2)
                        cells += 1
                    if lo + 1 < HEAD and (HEAD - lo) % 2 == 1:
                        path_tokens(lo + 1, lo + 3, cells)
                    if lo >= HEAD and (lo - HEAD) % PIECE == 0:
                        on_path(lo, min(lo + PIECE, SLOTS))
                        cells += 1
                    if lo + 1 >= HEAD and (lo + 1 - HEAD) % PIECE == 0 and lo + 1 < SLOTS:
                        path_tokens(lo + 1, min(lo + 1 + PIECE, SLOTS), cells)
                    if s == 2:
                        add_aligned(0)
                v.wait_ge(back_done, n)
                nc.vector.tensor_tensor_scan(Y[:, s, :], NL[:, s, :], enter[:, s % 2, :], bcarry[:, s + 1:s + 2],
                                             ALU.is_lt, ALU.add).then_inc(back_done, 1)
                n += 1
                scan_n = n
                if s:
                    steps_of(s - 1).then_inc(back_done, 1)
                    n += 1
            v.wait_ge(back_done, n)
            on_path(0, 2)
            path_tokens(0, 2, cells + 1)

            quantise(0)
            add_aligned(1)
            for n in range(NH):
                if n == 4:
                    quantise(1)
                clip_hidden(0, n)
            for g in range(NG):
                if g + 2 < NG:
                    add_aligned(g + 2)
                for n in range(NH):
                    if n == 4 and g + 2 < NG:
                        quantise(g + 2)
                    if g + 1 < NG:
                        clip_hidden(g + 1, n)
                    if n == 5:
                        finish(g, 0)
                finish(g, 1)

        @block.tensor
        def _(pe):
            pe.wait_ge(ident_made, 2)
            pe.wait_ge(ctx_loaded, 16)
            for b in range(2):
                for m in range(4):
                    q, k = 2 * b + m // KH, m % KH
                    mm = nc.tensor.transpose(bank01[b][:, m * P:m * P + P], S[:, q, k * P:k * P + P], ident[:, :])
                mm.then_inc(ctxT_done, 1)
            pe.wait_ge(pool_const, 1)
            pe.wait_ge(ctx_sq, 2)
            for q in range(NQ):
                for k in range(KH):
                    mm = nc.tensor.matmul(bank5[W * q:W * q + W, 0:P], ones[:, :], ST2[:, q, k, :],
                                          start=(k == 0), stop=(k == KH - 1))
            mm.then_inc(aa_done, 1)

            def dots(k):
                flat = dist_banks[k][:, :, :].rearrange("p a b -> p (a b)")
                for j in range(UL):
                    h = j // CL
                    if j % 2 == 0:
                        pe.wait_ge(xT_copied, (UL // 2) * k + j // 2 + 1)
                    for kk in range(KH):
                        for q in range(NQ):
                            mm = nc.tensor.matmul(flat[W * q:W * q + W, j * I:j * I + I],
                                                  XnT[:, k % 2, j, kk, W * q:W * q + W],
                                                  ST[:, q, kk, I * h:I * h + I], start=(kk == 0), stop=(kk == KH - 1))
                mm.then_inc(dot_done, 1)

            for k in range(LOADS):
                for j in range(UL // 2):
                    n = k * (UL // 2) + j
                    pe.wait_ge(xn_ready, UL * k + 2 * j + 2)
                    if n >= 2:
                        pe.wait_ge(xT_copied, n - 1)
                    for m in range(4):
                        mm = nc.tensor.transpose(bank01[n % 2][:, m * P:m * P + P],
                                                 Xn[:, k % 2, 2 * j + m // KH, (m % KH) * P:(m % KH) * P + P], ident[:, :])
                    mm.then_inc(xT_done, 1)
                dots(k)

            pe.wait_ge(pool_const, 7)
            pe.wait_ge(w_clip, 2 * NH)
            for n in range(NH):
                if n >= 2:
                    pe.wait_ge(wT_copied, n - 1)
                for m in range(4):
                    if n < NH // 2:
                        src = w1_q[:, 2 * n + m // KH, (m % KH) * P:(m % KH) * P + P]
                    else:
                        hh = 2 * (n - NH // 2) + m // OT
                        src = w2_q[:, m % OT, hh::NH]
                    mm = nc.tensor.transpose((flat4, path_ps)[n % 2][:, m * P:m * P + P], src, ident_bf[:, :])
                mm.then_inc(wT_done, 1)

            def path_T(g):
                pe.wait_ge(path_ready, PIECES + g)
                if g >= 1:
                    pe.wait_ge(path_copied, g)
                for half in range(2):
                    for j in range(2):
                        c = chunk_of(g) + j
                        for h in range(2):
                            at = (2 * j + h) * P
                            mm = nc.tensor.transpose(path_ps[I * half:I * half + I, at:at + P],
                                                     PT[:, c:c + I, CH * h + c], flip[:, :])
                mm.then_inc(pathT_done, 1)

            def align(g, h):
                pe.wait_ge(path_copied, g + 1)
                if g >= 1:
                    pe.wait_ge(x1_ready, 2 * (g - 1) + h + 1)
                for j in range(2):
                    for q in range(NQ):
                        nc.tensor.matmul(bank23[h][W * q:W * q + W, j, :], PB[:, g % 2, j, h, W * q:W * q + W],
                                         S_hm[:, h, q, :], start=True, stop=False)
                    for q in range(NQ):
                        mm = nc.tensor.matmul(bank23[h][W * q:W * q + W, j, :],
                                              PB[I * h:I * h + I, g % 2, j, h, W * q:W * q + W],
                                              S_lo[I * h:I * h + I, q, :], start=False, stop=True)
                mm.then_inc(aligned, 1)

            def tokens_T(g):
                pe.wait_ge(quant_read, g + 1)
                if g >= 1:
                    pe.wait_ge(xqT_copied, g)
                for t in range(4):
                    for k in range(KH):
                        mm = nc.tensor.transpose(bank4[:, k, t * P:t * P + P], xq[:, g % 2, t, k * P:k * P + P],
                                                 ident_bf[:, :])
                mm.then_inc(xqT_done, 1)

            def hidden(g, n):
                if n == 0:
                    pe.wait_ge(xqT_copied, g + 1)
                if NH * g + n >= 2:
                    pe.wait_ge(h_rounded, NH * g + n - 1)
                for k in range(KH):
                    mm = nc.tensor.matmul(bank01[n % 2][:, :], w1T[:, k, n * P:n * P + P], xqT[:, g % 2, k, :],
                                          start=(k == 0), stop=(k == KH - 1))
                mm.then_inc(h_done, 1)

            def output(g, part):
                t, n0 = part // 2, (part % 2) * (NH // 2)
                if part == 0:
                    pe.wait_ge(hq_ready, NH * (g + 1))
                if g >= 1 and part % 4 == 0:
                    pe.wait_ge(res_ready, 2 * (g - 1) + part // 4 + 1)
                for n in range(n0, n0 + NH // 2):
                    mm = nc.tensor.matmul(bank67[t // 2][:, t % 2, :], hq[:, g % 2, n, t * P:t * P + P], w2T[:, n, :],
                                          start=(n == 0), stop=(n == NH - 1))
                if part % 4 == 3:
                    mm.then_inc(y_done, 1)

            pe.wait_ge(ctx_stacked, 64)
            pe.wait_ge(ctx_rest, 2 * NR)
            pe.wait_ge(pool_const, 8)
            pe.wait_ge(wT_copied, NH)
            for g in range(2):
                path_T(g)
                align(g, 0)
                align(g, 1)
            tokens_T(0)
            path_T(2)
            for n in range(NH):
                hidden(0, n)
                if n == 1:
                    align(2, 0)
                if n == 3:
                    align(2, 1)
                if n == 6:
                    tokens_T(1)
            for g in range(NG):
                for n in range(NH):
                    if g + 1 < NG:
                        hidden(g + 1, n)
                    output(g, n)
                    if g + 3 < NG:
                        if n == 0:
                            path_T(g + 3)
                        if n == 2 or n == 4:
                            align(g + 3, n // 4)
                    if g + 2 < NG and n == 6:
                        tokens_T(g + 2)


_INS = ['x', 'ctx_1024', 'L0_ffn_w1', 'L0_ffn_b1', 'L0_ffn_w2', 'L0_ffn_b2']


def kernel(**inputs):
    import numpy as _np
    import concourse.bacc as _bacc
    from concourse import mybir as _mybir
    from concourse.bass_utils import run_bass_kernel_spmd as _run

    nc = _bacc.Bacc("TRN2", target_bir_lowering=False, num_devices=1)
    arrays, args = {}, []
    for name in _INS:
        a = _np.ascontiguousarray(inputs[name])
        arrays[f"in_{name}_dram"] = a
        args.append(nc.dram_tensor(f"in_{name}_dram", a.shape, _mybir.dt.from_np(a.dtype), kind="ExternalInput").ap())
    args.append(nc.dram_tensor("out_dram", (B, T, D), _mybir.dt.float32, kind="ExternalOutput").ap())
    align_ffn_kernel(nc, *args)
    r = _run(nc, [arrays], core_ids=[0])
    return r.results[0]["out_dram"]
```

```python
import concourse.bass as bass
from concourse import mybir
from contextlib import ExitStack

BIG = 1e30
B, T, D = 8, 512, 256
I = 64
HID = 1024
P = 128
W = 32
CH = T // W
NQ = P // W
NU = 2 * CH
SLOTS = I + CH - 1
KH = D // P
EPS = 1e-5
LOADS = 4
CL = CH // LOADS
UL = 2 * CL
NG = NU // 4
HEAD = CH - 2
PIECE = 13
PIECES = (SLOTS - HEAD) // PIECE
NR = NQ * D // I
assert PIECES * PIECE == SLOTS - HEAD
NH = HID // P
OT = D // P
ACT_ONE, W_ONE = 16.0, 64.0
WARM = (10, 2, 8, 4)
QMAX, QMIN = 127.0, -128.0


def align_ffn_kernel(nc: bass.Bass, x, ctx_in, w1, b1, w2, b2, out):
    f32, bf16, i16 = mybir.dt.float32, mybir.dt.bfloat16, mybir.dt.int16
    ALU, ACT = mybir.AluOpType, mybir.ActivationFunctionType

    x_v = x.rearrange("(q h) (c w) d -> q h w c d", h=2, w=W)
    out_v = out.rearrange("(q h) (c w) d -> q h w c d", h=2, w=W)
    ctx_v = ctx_in.rearrange("(q h) i d -> (h i) q d", h=2)

    with ExitStack() as ctx:
        def sb(name, shape, dt=f32):
            return ctx.enter_context(nc.sbuf_tensor(name, shape, dt))

        def bank(name, shape, dt=f32):
            return ctx.enter_context(nc.psum_tensor(name, shape, dt))

        def sem(name):
            return ctx.enter_context(nc.semaphore(name))

        X = sb("X", [P, NU, D])
        XT = sb("XT", [P, 2, UL, KH, P])
        stats = sb("stats", [P, NU, 6])
        mv = sb("mv", [P, NU, 2])
        std = sb("std", [P, NU])
        rstd = sb("rstd", [P, NU])
        var_eps = sb("var_eps", [P, NU])
        bb = sb("bb", [P, NU])
        rstd_m2 = sb("rstd_m2", [P, NU])
        S = sb("S", [P, NQ, D])
        S_hi = sb("S_hi", [P, NQ, D], bf16)
        S_hm = sb("S_hm", [P, 2, NQ, D], bf16)
        S_mid = sb("S_mid", [P, NQ, D], bf16)
        S_lo = sb("S_lo", [P, NQ, D], bf16)
        Sc = sb("Sc", [P, NQ, D])
        S_r1 = Sc
        ctx_stats = sb("ctx_stats", [P, NQ, 6])
        ctx_mv = sb("ctx_mv", [P, NQ, 2])
        ctx_len = sb("ctx_len", [P, NQ])
        ctx_lens = sb("ctx_lens", [P, NQ, W])
        ST = sb("ST", [P, NQ, KH, P])
        aa = sb("aa", [P, 2, I])
        prods = sb("prods", [P, 2, UL, I])
        norms = sb("norms", [P, 2, UL, I])
        E = sb("E", [P, SLOTS, NU])
        Dm = sb("Dm", [P, SLOTS, W + 1])
        M = sb("M", [P, SLOTS, W + 1])
        R = sb("R", [P, SLOTS + 1, W + 1])
        carry = sb("carry", [P, SLOTS + 1])
        init0 = sb("init0", [P, 1])
        NL = sb("NL", [P, SLOTS, W + 1], bf16)
        A = sb("A", [P, SLOTS, W], bf16)
        code = sb("code", [P, SLOTS, W], bf16)
        Y = sb("Y", [P, SLOTS, W + 1], bf16)
        enter = sb("enter", [P, 2, W + 1], bf16)
        bcarry = sb("bcarry", [P, SLOTS + 1], bf16)
        PT = sb("PT", [P, SLOTS, NU], bf16)
        chunk0 = sb("chunk0", [P, B])
        chunk15 = sb("chunk15", [P, B])
        first = sb("first", [P, 1])
        last = sb("last", [P, 1])
        ident = sb("ident", [P, P])
        table_in = sb("table_in", [P, 1])
        ident_bf = sb("ident_bf", [P, P], bf16)
        flip = sb("flip", [P, P], bf16)
        w1_raw = sb("w1_raw", [P, NH, D])
        w2_raw = sb("w2_raw", [P, OT, HID])
        w_int = sb("w_int", [P, 2, NH * D], i16)
        w1_q = w1_raw[:, :, :].rearrange("p n d -> p (n d)").bitcast(bf16)[:, 0:NH * D].rearrange(
            "p (n d) -> p n d", d=D)
        w2_q = w2_raw[:, :, :].rearrange("p n d -> p (n d)").bitcast(bf16)[:, 0:OT * HID].rearrange(
            "p (n d) -> p n d", d=HID)
        w1T = sb("w1T", [P, KH, HID], bf16)
        w2T = sb("w2T", [P, NH, D], bf16)
        b1_raw = sb("b1_raw", [P, NH])
        b1_int = sb("b1_int", [P, NH], i16)
        b1_q = sb("b1_q", [P, NH])
        b1_s = sb("b1_s", [P, NH])
        b2_raw = sb("b2_raw", [P, D])
        b2_int = sb("b2_int", [P, D], i16)
        b2_q = sb("b2_q", [P, D])
        b2_s = sb("b2_s", [P, D])
        PB = sb("PB", [P, 2, 2, 2, P], bf16)
        stats2 = sb("stats2", [P, NU, 6])
        mv2 = sb("mv2", [P, NU, 2])
        std2 = sb("std2", [P, NU])
        rstd2 = sb("rstd2", [P, NU])
        var_scaled = sb("var_scaled", [P, NU])
        xq_both = Dm[:, :, :].rearrange("p s w -> p (s w)")[:, 0:4 * D * 2]
        xq_int = xq_both[:, 0:4 * D].bitcast(i16).rearrange("p (a t d) -> p a t d", a=2, t=4)
        xq = xq_both[:, 4 * D:8 * D].bitcast(bf16).rearrange("p (a t d) -> p a t d", a=2, t=4)
        xqT = M[:, :, :].rearrange("p s w -> p (s w)")[:, 0:KH * 4 * P].bitcast(bf16).rearrange(
            "p (a k n) -> p a k n", a=2, k=KH)
        h_int = sb("h_int", [P, 2, NH, 4 * P], i16)
        hq = XT[:, :, :, :, :].rearrange("p a u k d -> p (a u k d)").bitcast(bf16).rearrange(
            "p (a n t) -> p a n t", a=2, n=NH)
        res = E[:, :, :].rearrange("p s u -> p (s u)")[:, 0:8 * D].rearrange("p (a t d) -> p a t d", a=2, t=4)

        bank01 = [bank("h0", [P, 512]), bank("h1", [P, 512])]
        bank23 = [bank("e0", [P, 2, D]), bank("e1", [P, 2, D])]
        bank4 = bank("t4", [P, 2, 4 * P], bf16)
        bank5 = bank("t5", [P, 512])
        bank67 = [bank("y0", [P, 2, D]), bank("y1", [P, 2, D])]
        path_ps = bank5[:, :].bitcast(bf16)
        flat4 = bank4[:, :, :].rearrange("p a b -> p (a b)")

        x_in = [sem(f"x_in{k}") for k in range(LOADS)]
        ctx_loaded = sem("ctx_loaded")
        w_loaded = sem("w_loaded")
        out_stored = [[sem(f"out_stored{a}{h}") for h in range(2)] for a in range(2)]
        ident_made = sem("ident_made")
        table_ready = sem("table_ready")
        pool_const = sem("pool_const")
        norms_made = sem("norms_made")
        prods_made = sem("prods_made")
        skewed = sem("skewed")
        clamped = sem("clamped")
        ctx_split = sem("ctx_split")
        ctx_rest = sem("ctx_rest")
        ctx_stacked = sem("ctx_stacked")
        w_clip = sem("w_clip")
        b_clip = sem("b_clip")
        biased = sem("biased")
        dve_order = sem("dve_order")
        var_ready = sem("var_ready")
        bb_ready = sem("bb_ready")
        ctx_centred = sem("ctx_centred")
        ctx_len_ready = sem("ctx_len_ready")
        squares_ready = sem("squares_ready")
        step_done = sem("step_done")
        back_done = sem("back_done")
        cells_done = sem("cells_done")
        path_ready = sem("path_ready")
        x1_ready = sem("x1_ready")
        var2_ready = sem("var2_ready")
        tokens_quantised = sem("tokens_quantised")
        hq_ready = sem("hq_ready")
        res_ready = sem("res_ready")
        std_ready = sem("std_ready")
        ctxT_copied = sem("ctxT_copied")
        aa_copied = sem("aa_copied")
        xT_copied = sem("xT_copied")
        rooted = sem("rooted")
        w_rounded = sem("w_rounded")
        wT_copied = sem("wT_copied")
        path_copied = sem("path_copied")
        std2_ready = sem("std2_ready")
        xqT_copied = sem("xqT_copied")
        h_rounded = sem("h_rounded")
        ctxT_done = sem("ctxT_done")
        aa_done = sem("aa_done")
        xT_done = sem("xT_done")
        dot_done = sem("dot_done")
        wT_done = sem("wT_done")
        pathT_done = sem("pathT_done")
        aligned = sem("aligned")
        xqT_done = sem("xqT_done")
        h_done = sem("h_done")
        y_done = sem("y_done")


        def tile_of(k, j):
            return CH * (j // CL) + CL * k + j % CL

        def by_half(ap):
            return ap.rearrange("p (h c) i -> p h c i", h=2)

        def chunk_of(g):
            return CH - 2 - 2 * g

        dist_banks = [bank23[0], bank23[1], bank67[0], bank67[1]]

        block = ctx.enter_context(nc.Block())

        @block.sync
        def _(sp):
            sp.dma_start(S[:, :, :], ctx_v).then_inc(ctx_loaded, 16)
            for k in range(LOADS):
                for h in range(2):
                    u0 = tile_of(k, CL * h)
                    for q in range(NQ):
                        sp.dma_start(X[W * q:W * q + W, u0:u0 + CL, :],
                                     x_v[q, h, :, CL * k:CL * k + CL, :]).then_inc(x_in[k], 16)
            sp.dma_start(w1_raw[:, :, :], w1.rearrange("(p n) d -> p n d", n=NH)).then_inc(w_loaded, 16)
            sp.dma_start(w2_raw[:, :, :], w2.rearrange("(n p) d -> p n d", p=P)).then_inc(w_loaded, 16)
            sp.dma_start(b2_raw[:, :], b2.partition_broadcast(P)).then_inc(w_loaded, 16)
            sp.dma_start(b1_raw[:, :], b1.rearrange("(p n) -> p n", n=NH)).then_inc(w_loaded, 16)
            sp.wait_ge(ctx_split, 2)
            for part, turned in ((S_hi, 0), (S_mid, 1)):
                for h in range(2):
                    at = I * (h ^ turned)
                    sp.dma_start(S_hm[at:at + I, h, :, :], part[I * h:I * h + I, :, :]).then_inc(ctx_stacked, 16)
            for g in range(NG):
                c0 = chunk_of(g)
                for h in range(2):
                    for j in range(2):
                        sp.wait_ge(res_ready, 4 * g + 2 * h + j + 1)
                        sp.dma_start(out_v[:, h, :, c0 + j, :], res[:, g % 2, 2 * h + j, :]).then_inc(out_stored[g % 2][h], 16)
            for a in range(2):
                for h in range(2):
                    sp.wait_ge(out_stored[a][h], 16 * 2 * (NG // 2))

        @block.gpsimd
        def _(pool):
            nc.gpsimd.memset(ident[:, :], 0.0).then_inc(ident_made, 1)
            pool.wait_ge(ident_made, 1)
            nc.gpsimd.affine_select(out=ident[:, :], in_=ident[:, :], compare_op=ALU.not_equal, fill=1.0, base=0,
                                    pattern=[[-1, P]], channel_multiplier=1).then_inc(ident_made, 1)
            nc.gpsimd.memset(ident_bf[:, :], 0.0).then_inc(pool_const, 1)
            nc.gpsimd.memset(flip[:, :], 0.0).then_inc(pool_const, 1)
            nc.gpsimd.memset(chunk0[:, :], 0.0).then_inc(pool_const, 1)
            nc.gpsimd.memset(chunk15[:, :], 0.0).then_inc(pool_const, 1)
            nc.gpsimd.memset(E[:, :, :], 0.0).then_inc(pool_const, 1)
            pool.wait_ge(pool_const, 5)
            nc.gpsimd.affine_select(out=ident_bf[:, :], in_=ident_bf[:, :], compare_op=ALU.not_equal, fill=1.0,
                                    base=0, pattern=[[-1, P]], channel_multiplier=1).then_inc(pool_const, 1)
            nc.gpsimd.affine_select(out=flip[:, :].rearrange("p (a b) -> p a b", b=W),
                                    in_=flip[:, :].rearrange("p (a b) -> p a b", b=W),
                                    compare_op=ALU.not_equal, fill=1.0, base=-(W - 1),
                                    pattern=[[-W, NQ], [1, W]], channel_multiplier=1).then_inc(pool_const, 1)
            for t, off in ((chunk0, 0), (chunk15, CH - 1)):
                nc.gpsimd.affine_select(out=t[:, :], in_=t[:, :], compare_op=ALU.not_equal, fill=1.0, base=-off,
                                        pattern=[[-CH, B]], channel_multiplier=1).then_inc(pool_const, 1)
            nc.gpsimd.memset(Dm[:, 0, 0:1], 0.0).then_inc(pool_const, 1)
            nc.gpsimd.memset(Dm[:, 1:SLOTS, 0:1], 0.0).then_inc(pool_const, 1)
            nc.gpsimd.memset(M[:, :, 0:1], BIG).then_inc(pool_const, 1)
            nc.gpsimd.memset(R[:, 0, :], BIG).then_inc(pool_const, 1)
            nc.gpsimd.memset(R[:, 1, 0:1], BIG).then_inc(pool_const, 1)
            nc.gpsimd.memset(NL[:, :, 0:1], 0.0).then_inc(pool_const, 1)
            nc.gpsimd.memset(enter[:, :, :], 0.0).then_inc(pool_const, 1)

            def add_products(k):
                pool.wait_ge(prods_made, k + 1)
                nc.gpsimd.tensor_tensor(norms[:, k % 2, :, :], norms[:, k % 2, :, :], prods[:, k % 2, :, :],
                                        ALU.add).then_inc(squares_ready, 1)

            pool.wait_ge(aa_copied, 1)
            for k in range(LOADS):
                pool.wait_ge(bb_ready, k + 1)
                if k >= 2:
                    pool.wait_ge(rooted, k - 1)
                nc.gpsimd.tensor_tensor(by_half(norms[:, k % 2, :, :]), aa[:, :, :].unsqueeze(2).to_broadcast([P, 2, CL, I]),
                                        by_half(bb[:, UL * k:UL * k + UL].unsqueeze(2)).to_broadcast([P, 2, CL, I]),
                                        ALU.add).then_inc(norms_made, 1)
                pool.wait_ge(norms_made, k + 1)
                add_products(k)

            pool.wait_ge(w_rounded, 4)
            nc.gpsimd.tensor_scalar(b1_q[:, :], b1_int[:, :], QMAX, QMIN, ALU.min, ALU.max).then_inc(b_clip, 1)
            nc.gpsimd.tensor_scalar(b2_q[:, :], b2_int[:, :], QMAX, QMIN, ALU.min, ALU.max).then_inc(b_clip, 1)
            pool.wait_ge(b_clip, 2)
            nc.gpsimd.tensor_scalar(b1_s[:, :], b1_q[:, :], ACT_ONE / W_ONE, 0.0, ALU.mult, ALU.add).then_inc(b_clip, 1)
            nc.gpsimd.tensor_scalar(b2_s[:, :], b2_q[:, :], 1.0 / W_ONE, 0.0, ALU.mult, ALU.add).then_inc(b_clip, 1)
            pool.wait_ge(b_clip, 4)

            for g in range(NG):
                c0 = chunk_of(g)
                pool.wait_ge(tokens_quantised, g + 1)
                for h in range(2):
                    v = X[:, CH * h + c0:CH * h + c0 + 2, :]
                    nc.gpsimd.tensor_tensor(v, v, b2_s[:, :].unsqueeze(1).to_broadcast([P, 2, D]),
                                            ALU.add).then_inc(biased, 1)

        @block.scalar
        def _(act):
            def roots(k):
                act.wait_ge(squares_ready, k + 1)
                nc.scalar.activation(norms[:, k % 2, :, :], norms[:, k % 2, :, :], ACT.Relu).then_inc(clamped, 1)
                act.wait_ge(clamped, k + 1)
                act.wait_ge(pool_const, 5)
                c0 = CL * k
                dst = bass.AP(E, c0 * NU + c0, [[SLOTS * NU, P], [CH, 2], [NU + 1, CL], [NU, I]])
                nc.scalar.activation(dst, by_half(norms[:, k % 2, :, :]), ACT.Sqrt).then_inc(rooted, 1)

            def spread(k):
                act.wait_ge(var_ready, k + 1)
                nc.scalar.activation(std[:, UL * k:UL * k + UL], var_eps[:, UL * k:UL * k + UL], ACT.Sqrt).then_inc(std_ready, 1)

            act.wait_ge(ident_made, 2)
            nc.scalar.activation(table_in[:, :], ident[:, 0:1], ACT.Sqrt).then_inc(table_ready, 1)

            def copy_xT(k, j):
                n = k * (UL // 2) + j
                act.wait_ge(xT_done, n + 1)
                if k >= 2 and j == 0:
                    act.wait_ge(dot_done, k - 1)
                nc.scalar.activation(XT[:, k % 2, 2 * j:2 * j + 2, :, :].rearrange("p u k n -> p (u k n)"),
                                     bank01[n % 2][:, :], ACT.Copy).then_inc(xT_copied, 1)

            for j in range(UL // 2):
                copy_xT(0, j)
            for b in range(2):
                act.wait_ge(ctxT_done, b + 1)
                nc.scalar.activation(ST[:, 2 * b:2 * b + 2, :, :].rearrange("p q k n -> p (q k n)"),
                                     bank67[b][:, :, :].rearrange("p j d -> p (j d)"),
                                     ACT.Copy).then_inc(ctxT_copied, 1)
            act.wait_ge(aa_done, 1)
            nc.scalar.activation(aa[:, :, :].rearrange("p h i -> p (h i)"), bank5[:, 0:P],
                                 ACT.Copy).then_inc(aa_copied, 1)
            spread(0)
            for j in range(UL // 2):
                copy_xT(1, j)
            spread(1)
            roots(0)
            spread(2)
            for j in range(UL // 2):
                copy_xT(2, j)
            roots(1)
            for j in range(UL // 2):
                copy_xT(3, j)
                if j == 2:
                    spread(3)
            roots(2)
            roots(3)

            nc.scalar.activation(S_hi[:, :, :], S[:, :, :], ACT.Copy).then_inc(ctx_split, 1)
            act.wait_ge(w_loaded, 64)
            nc.scalar.activation(w_int[:, 0, :], w1_raw[:, :, :].rearrange("p n d -> p (n d)"), ACT.Copy,
                                 scale=W_ONE).then_inc(w_rounded, 1)
            nc.scalar.activation(w_int[:, 1, :], w2_raw[:, :, :].rearrange("p n d -> p (n d)"), ACT.Copy,
                                 scale=W_ONE).then_inc(w_rounded, 1)
            nc.scalar.activation(b1_int[:, :], b1_raw[:, :], ACT.Copy, scale=W_ONE).then_inc(w_rounded, 1)
            nc.scalar.activation(b2_int[:, :], b2_raw[:, :], ACT.Copy, scale=W_ONE).then_inc(w_rounded, 1)
            act.wait_ge(ctx_rest, NR)
            nc.scalar.activation(S_mid[:, :, :], S_r1[:, :, :], ACT.Copy).then_inc(ctx_split, 1)
            for n in range(NH):
                act.wait_ge(wT_done, n + 1)
                src = (flat4, path_ps)[n % 2][:, 0:512]
                if n < NH // 2:
                    dst = w1T[:, :, 2 * n * P:2 * n * P + 2 * P].rearrange("p k (m n) -> p m k n", m=2)
                    src = src.rearrange("p (m k n) -> p m k n", m=2, k=KH)
                else:
                    m = n - NH // 2
                    dst = w2T[:, 2 * m:2 * m + 2, :].rearrange("p m n -> p (m n)")
                nc.scalar.activation(dst, src, ACT.Copy).then_inc(wT_copied, 1)

            def copy_path(g, j):
                if j == 0:
                    act.wait_ge(pathT_done, g + 1)
                    if g >= 2:
                        act.wait_ge(aligned, 2 * (g - 1))
                nc.scalar.activation(PB[:, g % 2, j, :, :].rearrange("p h n -> p (h n)"),
                                     path_ps[:, 2 * P * j:2 * P * j + 2 * P], ACT.Copy).then_inc(path_copied, 1)

            def deviation(g):
                act.wait_ge(var2_ready, g + 1)
                nc.scalar.activation(std2[:, 4 * g:4 * g + 4], var_scaled[:, 4 * g:4 * g + 4], ACT.Sqrt).then_inc(std2_ready, 1)

            def copy_xqT(g, k):
                if k == 0:
                    act.wait_ge(xqT_done, g + 1)
                    if g >= 2:
                        act.wait_ge(h_done, NH * (g - 1))
                nc.scalar.activation(xqT[:, g % 2, k, :], bank4[:, k, :], ACT.Copy).then_inc(xqT_copied, 1)

            def round_hidden(g, n):
                act.wait_ge(h_done, NH * g + n + 1)
                if g >= 2 and n == 0:
                    act.wait_ge(hq_ready, NH * (g - 1))
                nc.scalar.activation(h_int[:, g % 2, n, :], bank01[n % 2][:, :], ACT.Identity, bias=b1_s[:, n:n + 1],
                                     scale=1.0 / W_ONE).then_inc(h_rounded, 1)

            for g in range(2):
                for j in range(2):
                    copy_path(g, j)
            deviation(0)
            act.wait_ge(b_clip, 4)
            for m in range(2):
                copy_xqT(0, m)
            for m in range(2):
                copy_path(2, m)
            for n in range(NH):
                round_hidden(0, n)
                if n == 1:
                    deviation(1)
                if n in (4, 5):
                    copy_xqT(1, n - 4)
            for g in range(NG - 1):
                for n in range(NH):
                    round_hidden(g + 1, n)
                    if g + 3 < NG and n in (0, 1):
                        copy_path(g + 3, n)
                    if g + 2 < NG:
                        if n == 2:
                            deviation(g + 2)
                        if n in (5, 6):
                            copy_xqT(g + 2, n - 5)

        @block.vector
        def _(v):
            own = [0]

            def link(ins):
                own[0] += 1
                ins.then_inc(dve_order, 1)
                v.wait_ge(dve_order, own[0])

            v.wait_ge(ctx_loaded, 16)
            for q in range(NQ):
                nc.vector.bn_stats(ctx_stats[:, q, :], S[:, q, :]).then_inc(dve_order, 1)
            own[0] += NQ
            v.wait_ge(dve_order, own[0])
            for q in range(NQ):
                nc.vector.bn_aggr(ctx_mv[:, q, :], ctx_stats[:, q, :]).then_inc(dve_order, 1)
            own[0] += NQ
            v.wait_ge(dve_order, own[0])
            for q in range(NQ):
                nc.vector.tensor_scalar(Sc[:, q, :], S[:, q, :], ctx_mv[:, q, 0:1], None,
                                        ALU.subtract).then_inc(ctx_centred, 1)
            link(nc.vector.tensor_tensor(ctx_len[:, :], ctx_mv[:, :, 0], ctx_mv[:, :, 0], ALU.mult))
            link(nc.vector.tensor_tensor(ctx_len[:, :], ctx_len[:, :], ctx_mv[:, :, 1], ALU.add))
            nc.vector.tensor_scalar(ctx_lens[:, :, :], ctx_len[:, :].unsqueeze(2).to_broadcast([P, NQ, W]), float(D),
                                    None, ALU.mult).then_inc(ctx_len_ready, 1)

            v.wait_ge(pool_const, 16)
            nc.vector.reduce_max(first[:, :], chunk0[:, :], mybir.AxisListType.X).then_inc(dve_order, 1)
            nc.vector.reduce_max(last[:, :], chunk15[:, :], mybir.AxisListType.X).then_inc(dve_order, 1)
            own[0] += 2
            v.wait_ge(dve_order, own[0])
            nc.vector.tensor_scalar(init0[:, :], first[:, :], -BIG, BIG, ALU.mult, ALU.add).then_inc(dve_order, 1)
            nc.vector.tensor_scalar(Dm[:, 1:SLOTS, 0], Dm[:, 1:SLOTS, 0], 1.0, first[:, :], ALU.mult,
                                    ALU.add).then_inc(dve_order, 1)
            nc.vector.tensor_copy(bcarry[:, SLOTS:SLOTS + 1], last[:, :]).then_inc(dve_order, 1)
            own[0] += 3
            v.wait_ge(dve_order, own[0])
            link(nc.vector.tensor_scalar(Dm[:, 1:SLOTS, 0], Dm[:, 1:SLOTS, 0], BIG, None, ALU.mult))

            def distances(k):
                v.wait_ge(dot_done, k + 1)
                if k >= 2:
                    v.wait_ge(squares_ready, k - 1)
                flat = dist_banks[k][:, :, :].rearrange("p a b -> p (a b)")
                nc.vector.tensor_tensor(prods[:, k % 2, :, :], flat.rearrange("p (u i) -> p u i", i=I),
                                        rstd_m2[:, UL * k:UL * k + UL].unsqueeze(2).to_broadcast([P, UL, I]),
                                        ALU.mult).then_inc(prods_made, 1)

            def moments(k, j):
                if j == 0:
                    v.wait_ge(x_in[k], 16 * 2 * NQ)
                nc.vector.bn_stats(stats[:, UL * k + j, :], X[:, tile_of(k, j), :]).then_inc(dve_order, 1)
                own[0] += 1

            def variances(k):
                v.wait_ge(dve_order, own[0])
                for u in range(UL * k, UL * k + UL):
                    nc.vector.bn_aggr(mv[:, u, :], stats[:, u, :]).then_inc(dve_order, 1)
                own[0] += UL
                v.wait_ge(dve_order, own[0])
                nc.vector.tensor_scalar(var_eps[:, UL * k:UL * k + UL], mv[:, UL * k:UL * k + UL, 1], EPS, None,
                                        ALU.add).then_inc(var_ready, 1)

            def statistics(k):
                for j in range(UL):
                    moments(k, j)
                variances(k)

            def scales(k):
                us = slice(UL * k, UL * k + UL)
                v.wait_ge(std_ready, k + 1)
                link(nc.vector.reciprocal(rstd[:, us], std[:, us]))
                nc.vector.tensor_tensor(bb[:, us], mv[:, us, 1], rstd[:, us], ALU.mult).then_inc(dve_order, 1)
                nc.vector.tensor_scalar(rstd_m2[:, us], rstd[:, us], -2.0, None, ALU.mult).then_inc(dve_order, 1)
                own[0] += 2
                v.wait_ge(dve_order, own[0])
                nc.vector.scalar_tensor_tensor(out=bb[:, us], in0=bb[:, us], scalar=float(D),
                                               in1=rstd[:, us], op0=ALU.mult, op1=ALU.mult).then_inc(bb_ready, 1)

            def to_chunks(k):
                lo, hi = CL * k, (CL * k + CL if k + 1 < LOADS else SLOTS)
                v.wait_ge(rooted, k + 1)
                nc.vector.transpose(Dm[:, lo:hi, 1:W + 1], E[:, lo:hi, :]).then_inc(skewed, 1)

            right = [W - 1] + list(range(W - 1))
            left = list(range(1, W)) + [0]

            def not_left(s):
                return nc.vector.tensor_tensor(NL[:, s, 1:W + 1], M[:, s, W:0:-1], R[:, s + 1, W - 1::-1], ALU.is_le)

            def diagonal(s):
                return nc.vector.tensor_tensor(A[:, s, :], R[:, s, W - 1::-1], M[:, s, W:0:-1], ALU.is_le)

            steps = [0]
            scan_at = []

            def signal(ins):
                steps[0] += 1
                ins.then_inc(step_done, 1)

            def forward(lo, hi, loads):
                v.wait_ge(skewed, loads)
                for s in range(lo, hi):
                    if s:
                        v.wait_ge(step_done, scan_at[s - 1])
                    signal(nc.vector.tensor_tensor(M[:, s, 1:W + 1], R[:, s, 1:W + 1], R[:, s, 0:W], ALU.min))
                    if s:
                        signal(nc.vector.stream_shuffle(carry[:, s:s + 1], R[:, s, W:W + 1], right))
                    ready = steps[0]
                    if s >= 2:
                        signal(diagonal(s - 2))
                    if s < CL:
                        moments(LOADS - 1, 2 * s)
                    v.wait_ge(step_done, ready)
                    if s == 0:
                        signal(nc.vector.tensor_tensor_scan(R[:, 1, 1:W + 1], M[:, 0, 1:W + 1], Dm[:, 0, 1:W + 1],
                                                            init0[:, :], ALU.min, ALU.add))
                    else:
                        signal(nc.vector.tensor_tensor_scan(R[:, s + 1, :], M[:, s, :], Dm[:, s, :],
                                                            carry[:, s:s + 1], ALU.min, ALU.add))
                    scan_at.append(steps[0])
                    if s >= 2:
                        signal(not_left(s - 2))
                    if s < CL:
                        moments(LOADS - 1, 2 * s + 1)

            statistics(0)
            statistics(1)
            scales(0)
            distances(0)
            statistics(2)
            scales(1)
            scales(2)
            distances(1)
            to_chunks(0)
            forward(0, CL, 1)
            variances(3)
            distances(2)
            to_chunks(1)
            forward(CL, CL + 2, 2)
            scales(3)
            forward(CL + 2, 2 * CL, 2)
            distances(3)
            to_chunks(2)
            forward(2 * CL, 3 * CL, 3)
            to_chunks(3)
            forward(3 * CL, SLOTS, 4)
            v.wait_ge(step_done, steps[0])
            for s in (SLOTS - 2, SLOTS - 1):
                signal(diagonal(s))
                signal(not_left(s))
            v.wait_ge(step_done, steps[0])

            def steps_of(s):
                return nc.vector.scalar_tensor_tensor(out=code[:, s, :], in0=A[:, s, :], scalar=1.0,
                                                      in1=NL[:, s, 1:W + 1], op0=ALU.add, op1=ALU.mult)

            def on_path(lo, hi):
                nc.vector.tensor_scalar(A[:, lo:hi, :], Y[:, lo:hi, 0:W], 1.0, None, ALU.is_equal).then_inc(cells_done, 1)

            def path_tokens(lo, hi, count):
                v.wait_ge(cells_done, count)
                nc.vector.transpose(PT[:, lo:hi, :], A[:, lo:hi, :]).then_inc(path_ready, 1)

            S_f, S_hi_f, S_mid_f, S_lo_f, S_r1_f = (t[:, :, :].rearrange("p q d -> p (q d)")
                                                    for t in (S, S_hi, S_mid, S_lo, S_r1))

            def split_piece(i):
                if i == 0:
                    v.wait_ge(ctx_split, 1)
                    v.wait_ge(ctxT_done, 2)
                at = slice(I * i, I * i + I)
                nc.vector.tensor_tensor(S_r1_f[:, at], S_f[:, at], S_hi_f[:, at], ALU.subtract).then_inc(ctx_rest, 1)

            def rest_piece(i):
                if i == 0:
                    v.wait_ge(ctx_split, 2)
                at = slice(I * i, I * i + I)
                nc.vector.tensor_tensor(S_lo_f[:, at], S_r1_f[:, at], S_mid_f[:, at], ALU.subtract).then_inc(ctx_rest, 1)

            def clip_piece(i):
                if i == 0:
                    v.wait_ge(w_rounded, 4)
                half, at = i // NH, slice(D * (i % NH), D * (i % NH) + D)
                dst = (w1_q, w2_q)[half].rearrange("p a b -> p (a b)")
                nc.vector.tensor_scalar(dst[:, at], w_int[:, half, at], QMAX, QMIN, ALU.min, ALU.max).then_inc(w_clip, 1)

            def add_aligned(g):
                c0 = chunk_of(g)
                for h in range(2):
                    v.wait_ge(aligned, 2 * g + h + 1)
                    xv = X[:, CH * h + c0:CH * h + c0 + 2, :]
                    nc.vector.tensor_tensor(xv, bank23[h][:, :, :], xv, ALU.add).then_inc(x1_ready, 1)
                for h in range(2):
                    v.wait_ge(x1_ready, 2 * g + h + 1)
                    for j in range(2):
                        nc.vector.bn_stats(stats2[:, 4 * g + 2 * h + j, :], X[:, CH * h + c0 + j, :]).then_inc(dve_order, 1)
                own[0] += 4
                v.wait_ge(dve_order, own[0])
                for t in range(4):
                    nc.vector.bn_aggr(mv2[:, 4 * g + t, :], stats2[:, 4 * g + t, :]).then_inc(dve_order, 1)
                own[0] += 4
                v.wait_ge(dve_order, own[0])
                nc.vector.tensor_scalar(var_scaled[:, 4 * g:4 * g + 4], mv2[:, 4 * g:4 * g + 4, 1], EPS,
                                        1.0 / (ACT_ONE * ACT_ONE), ALU.add, ALU.mult).then_inc(var2_ready, 1)

            def quantise(g):
                c0 = chunk_of(g)
                v.wait_ge(std2_ready, g + 1)
                link(nc.vector.reciprocal(rstd2[:, 4 * g:4 * g + 4], std2[:, 4 * g:4 * g + 4]))
                for h in range(2):
                    for j in range(2):
                        t = 2 * h + j
                        nc.vector.tensor_scalar(xq_int[:, g % 2, t, :], X[:, CH * h + c0 + j, :],
                                                mv2[:, 4 * g + t, 0:1], rstd2[:, 4 * g + t:4 * g + t + 1],
                                                ALU.subtract, ALU.mult).then_inc(dve_order, 1)
                own[0] += 4
                v.wait_ge(dve_order, own[0])
                if g >= 2:
                    v.wait_ge(xqT_done, g - 1)
                nc.vector.tensor_scalar(xq[:, g % 2, :, :], xq_int[:, g % 2, :, :], QMIN, QMAX, ALU.max,
                                        ALU.min).then_inc(tokens_quantised, 1)

            def clip_hidden(g, n):
                v.wait_ge(h_rounded, NH * g + n + 1)
                if g >= 2 and n == 0:
                    v.wait_ge(y_done, 4 * (g - 1))
                nc.vector.tensor_scalar(hq[:, g % 2, n, :], h_int[:, g % 2, n, :], 0.0, QMAX, ALU.max,
                                        ALU.min).then_inc(hq_ready, 1)

            def finish(g, t0, t1):
                h = t0 // 2
                u0 = CH * h + chunk_of(g) + t0 % 2
                v.wait_ge(y_done, 4 * g + 2 * h + 2)
                v.wait_ge(biased, 2 * g + h + 1)
                if g >= 2:
                    v.wait_ge(out_stored[g % 2][h], 16 * 2 * (g // 2))
                nc.vector.scalar_tensor_tensor(
                    out=res[:, g % 2, t0:t1, :].rearrange("p j d -> p (j d)"),
                    in0=bank67[h][:, t0 % 2:t0 % 2 + t1 - t0, :].rearrange("p j d -> p (j d)"),
                    scalar=1.0 / (ACT_ONE * W_ONE),
                    in1=X[:, u0:u0 + t1 - t0, :].rearrange("p j d -> p (j d)"),
                    op0=ALU.mult, op1=ALU.add).then_inc(res_ready, t1 - t0)

            steps_of(SLOTS - 1).then_inc(back_done, 1)
            n = 1
            scan_n = 0
            cells = 0
            for s in range(SLOTS - 1, -1, -1):
                if s < SLOTS - 1:
                    v.wait_ge(back_done, scan_n)
                    nc.vector.scalar_tensor_tensor(out=enter[:, s % 2, 0:W], in0=Y[:, s + 1, 0:W], scalar=1.0,
                                                   in1=code[:, s + 1, :], op0=ALU.is_equal,
                                                   op1=ALU.mult).then_inc(back_done, 1)
                    nc.vector.stream_shuffle(bcarry[:, s + 1:s + 2], Y[:, s + 1, W:W + 1], left).then_inc(back_done, 1)
                    n += 2
                    i = SLOTS - 2 - s
                    if i < NR:
                        split_piece(i)
                    elif NR + 4 <= i < 2 * NR + 4:
                        rest_piece(i - NR - 4)
                    elif 2 * NR + 4 <= i < 2 * NR + 4 + 2 * NH:
                        clip_piece(i - 2 * NR - 4)
                    lo = s + 1
                    if lo < HEAD and (HEAD - lo) % 2 == 0:
                        on_path(lo, lo + 2)
                        cells += 1
                    if lo + 1 < HEAD and (HEAD - lo) % 2 == 1:
                        path_tokens(lo + 1, lo + 3, cells)
                    if lo >= HEAD and (lo - HEAD) % PIECE == 0:
                        on_path(lo, min(lo + PIECE, SLOTS))
                        cells += 1
                    if lo + 1 >= HEAD and (lo + 1 - HEAD) % PIECE == 0 and lo + 1 < SLOTS:
                        path_tokens(lo + 1, min(lo + 1 + PIECE, SLOTS), cells)
                    if s == 7:
                        add_aligned(0)
                    if s == 6:
                        quantise(0)
                    if s == 5:
                        add_aligned(1)
                    if s == 4:
                        quantise(1)
                    if s < 3:
                        clip_hidden(0, 2 - s)
                v.wait_ge(back_done, n)
                nc.vector.tensor_tensor_scan(Y[:, s, :], NL[:, s, :], enter[:, s % 2, :], bcarry[:, s + 1:s + 2],
                                             ALU.is_lt, ALU.add).then_inc(back_done, 1)
                n += 1
                scan_n = n
                if s:
                    steps_of(s - 1).then_inc(back_done, 1)
                    n += 1
            v.wait_ge(back_done, n)
            on_path(0, 2)
            path_tokens(0, 2, cells + 1)

            for n in range(3, NH):
                clip_hidden(0, n)
            for g in range(NG):
                if g + 2 < NG:
                    add_aligned(g + 2)
                for n in range(NH):
                    if n == 1 and g + 2 < NG:
                        quantise(g + 2)
                    if g + 1 < NG:
                        clip_hidden(g + 1, n)
                    if n == 4:
                        finish(g, 0, 2)
                if g + 1 < NG:
                    finish(g, 2, 4)
                else:
                    finish(g, 2, 3)
                    finish(g, 3, 4)

        @block.tensor
        def _(pe):
            pe.wait_ge(ident_made, 2)

            def ctx_T():
                pe.wait_ge(ctx_centred, NQ)
                for b in range(2):
                    flat = bank67[b][:, :, :].rearrange("p j d -> p (j d)")
                    for m in range(4):
                        q, k = 2 * b + m // KH, m % KH
                        mm = nc.tensor.transpose(flat[:, m * P:m * P + P], Sc[:, q, k * P:k * P + P], ident[:, :])
                    mm.then_inc(ctxT_done, 1)
                pe.wait_ge(ctx_len_ready, 1)
                for q in range(NQ):
                    mm = nc.tensor.matmul(bank5[W * q:W * q + W, 0:P], ctx_lens[:, q, :], ident[:, :],
                                          start=True, stop=True)
                mm.then_inc(aa_done, 1)

            def dots(k):
                flat = dist_banks[k][:, :, :].rearrange("p a b -> p (a b)")
                for j in range(UL):
                    h = j // CL
                    if j % 2 == 0:
                        pe.wait_ge(xT_copied, (UL // 2) * k + j // 2 + 1)
                    for kk in range(KH):
                        for q in range(NQ):
                            mm = nc.tensor.matmul(flat[W * q:W * q + W, j * I:j * I + I],
                                                  XT[:, k % 2, j, kk, W * q:W * q + W],
                                                  ST[:, q, kk, I * h:I * h + I], start=(kk == 0), stop=(kk == KH - 1))
                mm.then_inc(dot_done, 1)

            for k in range(LOADS):
                for j in range(UL // 2):
                    n = k * (UL // 2) + j
                    if j == 0:
                        pe.wait_ge(x_in[k], 16 * 2 * NQ)
                    if n >= 2:
                        pe.wait_ge(xT_copied, n - 1)
                    for m in range(4):
                        mm = nc.tensor.transpose(bank01[n % 2][:, m * P:m * P + P],
                                                 X[:, tile_of(k, 2 * j + m // KH), (m % KH) * P:(m % KH) * P + P],
                                                 ident[:, :])
                    mm.then_inc(xT_done, 1)
                if k == 0:
                    ctx_T()
                    pe.wait_ge(ctxT_copied, 2)
                dots(k)

            pe.wait_ge(pool_const, 6)
            pe.wait_ge(w_clip, 2 * NH)
            for n in range(NH):
                if n >= 2:
                    pe.wait_ge(wT_copied, n - 1)
                for m in range(4):
                    if n < NH // 2:
                        src = w1_q[:, 2 * n + m // KH, (m % KH) * P:(m % KH) * P + P]
                    else:
                        hh = 2 * (n - NH // 2) + m // OT
                        src = w2_q[:, m % OT, hh::NH]
                    mm = nc.tensor.transpose((flat4, path_ps)[n % 2][:, m * P:m * P + P], src, ident_bf[:, :])
                mm.then_inc(wT_done, 1)

            def path_T(g):
                pe.wait_ge(path_ready, PIECES + g)
                if g >= 1:
                    pe.wait_ge(path_copied, 2 * g)
                for half in range(2):
                    for j in range(2):
                        c = chunk_of(g) + j
                        for h in range(2):
                            at = (2 * j + h) * P
                            mm = nc.tensor.transpose(path_ps[I * half:I * half + I, at:at + P],
                                                     PT[:, c:c + I, CH * h + c], flip[:, :])
                mm.then_inc(pathT_done, 1)

            def align(g, h):
                pe.wait_ge(path_copied, 2 * (g + 1))
                if g >= 1:
                    pe.wait_ge(x1_ready, 2 * (g - 1) + h + 1)
                for j in range(2):
                    for q in range(NQ):
                        nc.tensor.matmul(bank23[h][W * q:W * q + W, j, :], PB[:, g % 2, j, h, W * q:W * q + W],
                                         S_hm[:, h, q, :], start=True, stop=False)
                    for q in range(NQ):
                        mm = nc.tensor.matmul(bank23[h][W * q:W * q + W, j, :],
                                              PB[I * h:I * h + I, g % 2, j, h, W * q:W * q + W],
                                              S_lo[I * h:I * h + I, q, :], start=False, stop=True)
                mm.then_inc(aligned, 1)

            def tokens_T(g):
                pe.wait_ge(tokens_quantised, g + 1)
                if g >= 1:
                    pe.wait_ge(xqT_copied, 2 * g)
                for t in range(4):
                    for k in range(KH):
                        mm = nc.tensor.transpose(bank4[:, k, t * P:t * P + P], xq[:, g % 2, t, k * P:k * P + P],
                                                 ident_bf[:, :])
                mm.then_inc(xqT_done, 1)

            def hidden(g, n):
                if n == 0:
                    pe.wait_ge(xqT_copied, 2 * (g + 1))
                if NH * g + n >= 2:
                    pe.wait_ge(h_rounded, NH * g + n - 1)
                for k in range(KH):
                    mm = nc.tensor.matmul(bank01[n % 2][:, :], w1T[:, k, n * P:n * P + P], xqT[:, g % 2, k, :],
                                          start=(k == 0), stop=(k == KH - 1))
                mm.then_inc(h_done, 1)

            def output(g, part):
                t, n0 = part // 2, (part % 2) * (NH // 2)
                if part < 2:
                    pe.wait_ge(hq_ready, NH * g + n0 + NH // 2)
                if g >= 1 and part % 4 == 0:
                    pe.wait_ge(res_ready, 4 * (g - 1) + t + 2)
                for n in range(n0, n0 + NH // 2):
                    mm = nc.tensor.matmul(bank67[t // 2][:, t % 2, :], hq[:, g % 2, n, t * P:t * P + P], w2T[:, n, :],
                                          start=(n == 0), stop=(n == NH - 1))
                if n0:
                    mm.then_inc(y_done, 1)

            pe.wait_ge(ctx_stacked, 64)
            pe.wait_ge(ctx_rest, 2 * NR)
            pe.wait_ge(pool_const, 7)
            pe.wait_ge(wT_copied, NH)
            def keep_warm(count):
                for i in range(count):
                    nc.tensor.matmul(bank67[0][:, :, :].rearrange("p j d -> p (j d)"), w1T[:, 0, 0:P], w1T[:, 0, 0:512],
                                     start=True, stop=True)

            keep_warm(WARM[0])
            for g in range(2):
                path_T(g)
                keep_warm(WARM[1])
                align(g, 0)
                align(g, 1)
            keep_warm(WARM[2])
            tokens_T(0)
            path_T(2)
            keep_warm(WARM[3])
            for n in range(NH):
                hidden(0, n)
                if n == 1:
                    align(2, 0)
                if n == 3:
                    align(2, 1)
                if n == 4:
                    tokens_T(1)
            for g in range(NG):
                for n in range(NH):
                    if g + 1 < NG:
                        hidden(g + 1, n)
                    if g + 3 < NG and n == 0:
                        path_T(g + 3)
                    output(g, n)
                    if g + 3 < NG and n in (2, 4):
                        align(g + 3, n // 4)
                    if g + 2 < NG and n == 5:
                        tokens_T(g + 2)


_INS = ['x', 'ctx_1024', 'L0_ffn_w1', 'L0_ffn_b1', 'L0_ffn_w2', 'L0_ffn_b2']


def kernel(**inputs):
    import numpy as _np
    import concourse.bacc as _bacc
    from concourse import mybir as _mybir
    from concourse.bass_utils import run_bass_kernel_spmd as _run

    nc = _bacc.Bacc("TRN2", target_bir_lowering=False, num_devices=1)
    arrays, args = {}, []
    for name in _INS:
        a = _np.ascontiguousarray(inputs[name])
        arrays[f"in_{name}_dram"] = a
        args.append(nc.dram_tensor(f"in_{name}_dram", a.shape, _mybir.dt.from_np(a.dtype), kind="ExternalInput").ap())
    args.append(nc.dram_tensor("out_dram", (B, T, D), _mybir.dt.float32, kind="ExternalOutput").ap())
    align_ffn_kernel(nc, *args)
    r = _run(nc, [arrays], core_ids=[0])
    return r.results[0]["out_dram"]
```
